# Optimizing a Trainium2 kernel written in Bass

```python
import numpy as np
import jax
import jax.numpy as jnp

def _softmax(x, axis=-1):
    return jax.nn.softmax(x, axis=axis)

def _gelu(x):
    return jax.nn.gelu(x, approximate=True)

def _silu(x):
    return jax.nn.silu(x)

def _sigmoid(x):
    return jax.nn.sigmoid(x)

def _layernorm(x, axis=-1, eps=1e-05):
    m = jnp.mean(x, axis=axis, keepdims=True)
    v = jnp.var(x, axis=axis, keepdims=True)
    return (x - m) / jnp.sqrt(v + eps)

def _scatter_add(tgt, idx, src, axis=0):
    return tgt.at[idx].add(src)

def _segment_sum(src, seg, n):
    return jax.ops.segment_sum(src, seg, n)
kernel_name = 'mk_adj_resnorm_d1_adj_r2_84905f'

def setup_inputs(seed: int=0):
    np.random.seed(seed)
    _w = jnp.asarray

    def _rec_inputs():
        import jax
        import jax.numpy as jnp
        _gk = jax.random.key(seed)
        x = -0.0004776 + 1.001 * jax.random.normal(jax.random.fold_in(_gk, 1), (2048, 512), jnp.float32)
        _a = jax.random.bernoulli(jax.random.fold_in(_gk, 2), 0.00195312, (2048, 2048))
        _a = jnp.logical_or(_a, jnp.eye(2048, dtype=bool))
        _af = _a.astype(jnp.float32)
        adj = _af
        return (x, adj)
    x, adj = _rec_inputs()

    def _L0_gnn_setup():
        import jax, jax.numpy as jnp
        import numpy as np
        N, H, E, HEADS = (1500, 512, 10000, 8)
        DK = H // HEADS
        key = jax.random.key(seed)
        k1, k2, k3, k4 = jax.random.split(key, 4)
        inst_feature = jax.random.normal(k1, (N, H), dtype=jnp.float32)
        rel_pair_index = jax.random.randint(k2, (E, 2), 0, N, dtype=jnp.int64)
        agg = jnp.zeros((N, N), dtype=jnp.float32)
        agg = agg.at[rel_pair_index[:, 0], rel_pair_index[:, 1]].set(1.0)
        agg = agg.at[jnp.arange(N), jnp.arange(N)].set(1.0)
        std = float(np.sqrt(2.0 / (H + DK)))
        Wq = jax.random.normal(k3, (H, H), dtype=jnp.float32) * std
        Wk = jax.random.normal(k4, (H, H), dtype=jnp.float32) * std
        bq = jnp.zeros((H,), dtype=jnp.float32)
        bk = jnp.zeros((H,), dtype=jnp.float32)
        return {'inst_feature': inst_feature, 'aggregator_matrix': agg, 'rel_pair_index': rel_pair_index, 'Wq': Wq, 'bq': bq, 'Wk': Wk, 'bk': bk}
    _L0_gnn_all = _L0_gnn_setup()
    _L0_gnn_in = {k: v for k, v in _L0_gnn_all.items() if k in ('rel_pair_index', 'Wq', 'bq', 'Wk', 'bk')}
    del _L0_gnn_all
    return {'x': x, 'adj': adj, 'L0_gnn_rel_pair_index': _L0_gnn_in['rel_pair_index'], 'L0_gnn_Wq': _L0_gnn_in['Wq'], 'L0_gnn_bq': _L0_gnn_in['bq'], 'L0_gnn_Wk': _L0_gnn_in['Wk'], 'L0_gnn_bk': _L0_gnn_in['bk']}

def reference(x, adj, L0_gnn_rel_pair_index, L0_gnn_Wq, L0_gnn_bq, L0_gnn_Wk, L0_gnn_bk):
    import jax
    import jax.numpy as jnp

    def _L0_gnn_ref(inst_feature, aggregator_matrix, rel_pair_index, Wq, bq, Wk, bk):
        import jax, jax.numpy as jnp
        import numpy as np
        N, H, E, HEADS = (1500, 512, 10000, 8)
        DK = H // HEADS
        n = inst_feature.shape[0]
        sub = rel_pair_index[:, 0]
        obj = rel_pair_index[:, 1]
        q = (inst_feature[sub] @ Wq.T + bq).reshape(-1, HEADS, DK)
        k = (inst_feature[obj] @ Wk.T + bk).reshape(-1, HEADS, DK)
        att = ((q * k).sum(-1) / np.sqrt(DK)).T.astype(inst_feature.dtype)
        scores = jnp.zeros((HEADS, n, n), dtype=inst_feature.dtype)
        scores = scores.at[:, sub, obj].set(att)
        mask = (1.0 - aggregator_matrix).astype(bool)
        scores = jnp.where(mask[None], -jnp.inf, scores)
        di = jnp.arange(n)
        scores = scores.at[:, di, di].set(1e-07)
        attn = jax.nn.softmax(scores, axis=2)
        aggregator_factor = attn.sum(axis=0) / HEADS
        return aggregator_factor @ inst_feature
    x = _layernorm(x + _L0_gnn_ref(x, adj, L0_gnn_rel_pair_index, L0_gnn_Wq, L0_gnn_bq, L0_gnn_Wk, L0_gnn_bk), axis=-1)
    return x

_drawn_inputs = setup_inputs


def setup_inputs(seed=0):
    import zlib

    import numpy as np

    out = dict(_drawn_inputs(seed))
    spreads = {'L0_gnn_bq': (0.0, 2.0), 'L0_gnn_bk': (0.0, 2.0)}
    factors = {'L0_gnn_Wq': 57.049, 'L0_gnn_Wk': 76.9}
    for name, (base, spread) in spreads.items():
        noise = np.random.default_rng([zlib.crc32(name.encode()), seed]).standard_normal(out[name].shape)
        drawn = base * np.exp(spread * noise) if base else spread * noise
        out[name] = jnp.asarray(drawn.astype(out[name].dtype))
    for name, factor in factors.items():
        out[name] = (out[name] * factor).astype(out[name].dtype)
    return out
```

```python
import concourse.bass as bass
from concourse import mybir
from contextlib import ExitStack


class Chain:

    def __init__(self, engine, sem, base=0):
        self.engine, self.sem, self.base, self.n = engine, sem, base, 0

    def __call__(self, ins):
        self.n += 1
        ins.then_inc(self.sem, 1)
        self.engine.wait_ge(self.sem, self.base + self.n)


def gnn_attention_layernorm_kernel(
    nc: bass.Bass,
    x: bass.AP,
    adj: bass.AP,
    pairs: bass.AP,
    Wq: bass.AP,
    bq: bass.AP,
    Wk: bass.AP,
    bk: bass.AP,
    out: bass.AP,
):
    fp32, fp16, i32 = mybir.dt.float32, mybir.dt.float16, mybir.dt.int32
    ALU = mybir.AluOpType
    ACT = mybir.ActivationFunctionType
    AX = mybir.AxisListType

    P = 128
    N, H = x.shape
    T = N // P
    HT = H // P
    HEADS = 8
    DK = H // HEADS
    E = pairs.shape[0]
    EC = 80
    EP = E // EC
    assert EP * EC == E and EP <= P
    CH = -(-E // P)
    SELF = 1e-7
    EPS = 1e-5
    LO = 2048.0
    XG = 4
    OG = 4

    owner = nc.dram_tensor("owner", [N * N, 1], i32, kind="Internal").ap()
    adj_flat = adj.rearrange("a (b o) -> (a b) o", o=1)
    x_tiles = x.rearrange("(t p) h -> p t h", p=P)
    out_tiles = out.rearrange("(t p) h -> p t h", p=P)

    ctx = ExitStack()
    with ctx:
        def sb(name, shape, dt=fp32):
            return ctx.enter_context(nc.sbuf_tensor(name, shape, dt))

        def pb(name, shape, dt=fp32):
            return ctx.enter_context(nc.psum_tensor(name, shape, dt))

        def sem(name):
            return ctx.enter_context(nc.semaphore(name))

        ident = sb("ident", [P, P])
        ident16 = sb("ident16", [P, P], fp16)
        offdiag = sb("offdiag", [P, P])
        before = sb("before", [P, P])
        after = sb("after", [P, P])
        ones = sb("ones", [P, P])
        iota_f = sb("iota_f", [P, P])
        iota16 = sb("iota16", [P, P], fp16)
        slot0 = sb("slot0", [P, 1])
        chunk_lo = sb("chunk_lo", [P, CH])
        self_col = sb("self_col", [P, 1])
        xs = sb("xs", [P, T, H])
        xh = sb("xh", [P, T, H], fp16)
        xl = sb("xl", [P, T, H], fp16)
        adjf = sb("adjf", [P, 2, N])
        mask = sb("mask", [P, 2, N], fp16)
        maskT = sb("maskT", [P, 2, T, P], fp16)
        low_part = sb("low_part", [P, 2, H])
        ax = sb("ax", [P, T, H])
        wraw = ax[:, 0:2 * HT, :].rearrange("p (w o) i -> p w o i", w=2)
        rowsum = sb("rowsum", [P, T])
        wT = sb("wT", [P, 2, HT, H])
        bias = sb("bias", [P, 2, H])
        pr = sb("pr", [P, EC, 2], i32)
        prf = sb("prf", [P, EC, 2])
        so16 = sb("so16", [P, EC, 3], fp16)
        keyf = sb("keyf", [P, EC])
        key_i = sb("key_i", [P, EC], i32)
        adjv = sb("adjv", [P, EC])
        act = sb("act", [P, EC])
        incl = sb("incl", [P, EC])
        zeros80 = sb("zeros80", [P, EC])
        slot = sb("slot", [P, EC])
        slot16 = sb("slot16", [P, EC], fp16)
        offs = sb("offs", [P, 2])
        nch_f = sb("nch_f", [P, 2])
        nch_i = sb("nch_i", [P, 1], i32)
        chunk_tmp = sb("chunk_tmp", [P, CH])
        area = sb("area", [P, 5120])
        diff = area[:, 0:2 * XG * H].rearrange("p (b n) -> p b n", b=2)
        onehot = area[:, :].bitcast(fp16).rearrange("p (c s) -> p c s", s=P)
        gT = area[:, 0:2 * HT * P].rearrange("p (w k e) -> p w k e", w=2, k=HT)
        qk = area[:, 1024:1024 + 3 * H].rearrange("p (w h) -> p w h", w=3)
        attB = area[:, 2560:2560 + HEADS * P].rearrange("p (h e) -> p h e", h=HEADS)
        attM = area[:, 3584:3584 + HEADS * P].rearrange("p (h e) -> p h e", h=HEADS)
        wL = area[:, 0:T * P].rearrange("p (t e) -> p t e", t=T)
        g = sb("g", [P, 2, H])
        se = sb("se", [P, 3])
        si = sb("si", [P, 2], i32)
        split_i = sb("split_i", [P, 2], i32)
        split_f = sb("split_f", [P, 2])
        cols = sb("cols", [P, 16])
        keyv, subv, dup, cnt, rep, uniq = (cols[:, i:i + 1] for i in range(6))
        hiv, lov, objv, slotv, wcol, owned = (cols[:, i:i + 1] for i in range(6, 12))
        skey_f, k2 = cols[:, 12:13], cols[:, 13:14]
        skey_i = sb("skey_i", [P, 1], i32)
        obj_i = sb("obj_i", [P, 1], i32)
        own_g = sb("own_g", [P, 1], i32)
        own_f = sb("own_f", [P, 1])
        slot_i = sb("slot_i", [P, 1], i32)
        kb = sb("kb", [P, 2, P])
        same = sb("same", [P, P])
        junk = sb("junk", [P, P])
        att1 = sb("att1", [P, HEADS])
        seg = sb("seg", [P, HEADS])
        hot_lo = sb("hot_lo", [P, P])
        hot_hi = sb("hot_hi", [P, T])
        hot_loT = sb("hot_loT", [P, P])
        spread = sb("spread", [P, T, HEADS + 1])
        spread8 = sb("spread8", [P, T, HEADS])
        e9 = sb("e9", [P, HEADS + 1])
        dlt = sb("dlt", [P, HEADS])
        pexp = sb("pexp", [P, HEADS])
        att_all = sb("att_all", [P, CH, HEADS])
        p_all = sb("p_all", [P, CH, HEADS])
        col_all = sb("col_all", [P, CH, 6])
        m_st = sb("m_st", [P, T, HEADS])
        z_st = sb("z_st", [P, T, HEADS + 1])
        rz_st = sb("rz_st", [P, T, HEADS + 1])
        e0 = sb("e0", [P, T, HEADS])
        e1 = sb("e1", [P, T, HEADS])
        rt = sb("rt", [P, T, HEADS])
        n0 = sb("n0", [P, T])
        d1 = sb("d1", [P, T])
        yb = sb("yb", [P, OG, H])
        stats = sb("stats", [P, OG, 6])
        mv = sb("mv", [P, OG, 2])
        std = sb("std", [P, OG])
        rstd = sb("rstd", [P, OG])
        shift = sb("shift", [P, OG])

        tp = [pb(f"tp{i}", [P, T // 2, P], fp16) for i in range(2)]
        hi_ps = [pb(f"hi_ps{i}", [P, H]) for i in range(2)]
        lo_ps = [pb(f"lo_ps{i}", [P, H]) for i in range(2)]
        ea = pb("ea", [P, H])
        eb = pb("eb", [P, H])

        names = """pairs_in x_in0 x_in1 x_in2 x_in3 adj_in0 adj_in1 w_in bias_in const_pool const_dve
            xh_done diff_done xl_done w_tr w_copied keys_done adjv_in
            mask_done tr0_done tr1_done copy0_done copy1_done mm_done low_done ax_done
            act_sum_done offs_done nch_done
            onehot_done compact_done idx_done sub_rows_in obj_rows_in kb_done keyT_done keyT_used skey_done
            owner_out subT_done subT_copied objT_done objT_copied q_done k_done attB_done attT_done
            maxspread_done max_done
            hotlo_done hotloT_done hotloT_copied mG_done dlt_done exp_done zspread_done z_done key2_done owner_in
            m_final row_exp_done d1_done scaled_done
            obj2_done obj2_rows_in rzG_done wL_done edge_mm_done edge_added hotlo3_done hotloT3_done hotloT3_copied
            var_done std_done norm_ready act_norm_done dve_norm_done out_done
            dve_setup dve_head dve_tile dve_flags dve_scan dve_max dve_exp dve_rows dve_edges dve_norm
            """.split()
        S = type("S", (), {})
        S = {n: sem(n) for n in names}

        block = ctx.enter_context(nc.Block())

        @block.sync
        def _(sp):
            sp.dma_start(pr[0:EP], pairs.rearrange("(p c) w -> p c w", p=EP)).then_inc(S["pairs_in"], 16)
            sp.dma_start(adjf[:, 0, :], adj[0:P, :]).then_inc(S["adj_in0"], 16)
            for i in range(T // XG):
                sp.dma_start(xs[:, i * XG:(i + 1) * XG, :],
                             x_tiles[:, i * XG:(i + 1) * XG, :]).then_inc(S[f"x_in{i}"], 16)
            sp.dma_start(adjf[:, 1, :], adj[P:2 * P, :]).then_inc(S["adj_in1"], 16)
            for w, src in enumerate((Wq, Wk)):
                sp.dma_start(wraw[:, w, :, :], src.rearrange("(o p) i -> p o i", p=P)).then_inc(S["w_in"], 16)
            for w, src in enumerate((bq, bk)):
                sp.dma_start(bias[:, w, :], src.partition_broadcast(P)).then_inc(S["bias_in"], 16)
            with sp.Fori(2, T - 1, 2) as t:
                for b in range(2):
                    sp.wait_ge(S["mask_done"], t + b - 1)
                    sp.dma_start(adjf[:, b, :], adj[bass.ds((t + b) * P, P), :]).then_inc(S[f"adj_in{b}"], 16)
            with sp.Fori(0, T // OG) as k:
                sp.wait_ge(S["act_norm_done"], k + 2)
                sp.wait_ge(S["dve_norm_done"], k + 2)
                sp.dma_start(out_tiles[:, bass.ds(k * OG, OG), :],
                             ax[:, bass.ds(k * OG, OG), :]).then_inc(S["out_done"], 16)
            sp.wait_ge(S["out_done"], 16 * (T // OG))

        @block.gpsimd
        def _(pool):
            nc.gpsimd.memset(ones[:, :], 1.0).then_inc(S["const_pool"], 1)
            nc.gpsimd.iota(iota_f[:, :], [[1, P]], base=0, channel_multiplier=0,
                           allow_small_or_imprecise_dtypes=True).then_inc(S["const_pool"], 1)
            nc.gpsimd.iota(slot0[:, :], [[0, 1]], base=0, channel_multiplier=1,
                           allow_small_or_imprecise_dtypes=True).then_inc(S["const_pool"], 1)
            nc.gpsimd.iota(chunk_lo[:, :], [[P, CH]], base=0, channel_multiplier=0,
                           allow_small_or_imprecise_dtypes=True).then_inc(S["const_pool"], 1)
            pool.wait_ge(S["const_pool"], 4)
            nc.gpsimd.affine_select(out=ident[:, :], in_=ones[:, :], compare_op=ALU.is_equal, fill=0.0, base=0,
                                    pattern=[[-1, P]], channel_multiplier=1).then_inc(S["const_pool"], 1)
            nc.gpsimd.affine_select(out=offdiag[:, :], in_=ones[:, :], compare_op=ALU.not_equal, fill=0.0, base=0,
                                    pattern=[[-1, P]], channel_multiplier=1).then_inc(S["const_pool"], 1)
            nc.gpsimd.affine_select(out=before[:, :], in_=ones[:, :], compare_op=ALU.is_gt, fill=0.0, base=0,
                                    pattern=[[-1, P]], channel_multiplier=1).then_inc(S["const_pool"], 1)
            nc.gpsimd.affine_select(out=after[:, :], in_=ones[:, :], compare_op=ALU.is_gt, fill=0.0, base=0,
                                    pattern=[[1, P]], channel_multiplier=-1).then_inc(S["const_pool"], 1)
            pool.wait_ge(S["keys_done"], 1)
            for j in range(EC):
                pool.indirect_dma_start(
                    out=adjv[0:EP, j:j + 1], out_offset=None, in_=adj_flat[:, :],
                    in_offset=bass.IndirectOffsetOnAxis(ap=key_i[0:EP, j:j + 1], axis=0),
                ).then_inc(S["adjv_in"], 16)
            pool.wait_ge(S["nch_done"], 1)
            nch = pool.value_load(nch_i[0:1, 0:1], min_val=1, max_val=CH)
            last_pair = pool.to_reg(N * N - 1)
            with pool.Fori(1, nch + 1) as turn:
                pool.wait_ge(S["nch_done"], 1)
                pool.wait_ge(S["idx_done"], turn)
                for w, s in enumerate(("sub_rows_in", "obj_rows_in")):
                    pool.indirect_dma_start(
                        out=g[:, w, :], out_offset=None, in_=x[:, :],
                        in_offset=bass.IndirectOffsetOnAxis(ap=si[:, w:w + 1], axis=0)).then_inc(S[s], 16)
                pool.wait_ge(S["nch_done"], 1)
                pool.wait_ge(S["skey_done"], turn)
                pool.indirect_dma_start(
                    out=owner, out_offset=bass.IndirectOffsetOnAxis(ap=skey_i[:, :], axis=0), in_=slot_i[:, :],
                    in_offset=None, bounds_check=last_pair, oob_is_err=False).then_inc(S["owner_out"], 16)
                pool.wait_ge(S["owner_out"], 16 * turn)
            with pool.Fori(1, nch + 1) as turn:
                pool.wait_ge(S["nch_done"], 1)
                pool.wait_ge(S["key2_done"], turn)
                pool.indirect_dma_start(
                    out=own_g[:, :], out_offset=None, in_=owner,
                    in_offset=bass.IndirectOffsetOnAxis(ap=skey_i[:, :], axis=0),
                    bounds_check=last_pair, oob_is_err=False).then_inc(S["owner_in"], 16)
            with pool.Fori(1, nch + 1) as turn:
                pool.wait_ge(S["nch_done"], 1)
                pool.wait_ge(S["obj2_done"], turn)
                pool.indirect_dma_start(
                    out=g[:, 1, :], out_offset=None, in_=x[:, :],
                    in_offset=bass.IndirectOffsetOnAxis(ap=obj_i[:, :], axis=0)).then_inc(S["obj2_rows_in"], 16)

        @block.scalar
        def _(act_e):
            act_e.wait_ge(S["const_dve"], 1)
            nc.scalar.activation(std[:, 0:1], ident[:, 0:1], ACT.Copy).then_inc(S["act_norm_done"], 1)
            for i in range(T // XG):
                piece = slice(i * XG, (i + 1) * XG)
                act_e.wait_ge(S[f"x_in{i}"], 16)
                nc.scalar.activation(xh[:, piece, :], xs[:, piece, :], ACT.Copy).then_inc(S["xh_done"], 1)
                if i >= 1:
                    prev = slice((i - 1) * XG, i * XG)
                    act_e.wait_ge(S["diff_done"], i)
                    nc.scalar.activation(xl[:, prev, :].rearrange("p a b -> p (a b)"), diff[:, (i - 1) % 2, :],
                                         ACT.Copy, scale=LO).then_inc(S["xl_done"], 1)
            act_e.wait_ge(S["diff_done"], T // XG)
            nc.scalar.activation(xl[:, T - XG:T, :].rearrange("p a b -> p (a b)"),
                                 diff[:, (T // XG - 1) % 2, :], ACT.Copy, scale=LO).then_inc(S["xl_done"], 1)

            def copy_half(t, b):
                act_e.wait_ge(S["tr0_done"], t + 1)
                if not isinstance(t, int) or t >= 2:
                    act_e.wait_ge(S["mm_done"], t - 1)
                nc.scalar.activation(maskT[:, b, 0:T // 2, :], tp[0][:, :, :], ACT.Copy).then_inc(S["copy0_done"], 1)

            def low_out(t, b):
                act_e.wait_ge(S["mm_done"], t + 1)
                if not isinstance(t, int) or t >= 2:
                    act_e.wait_ge(S["ax_done"], t - 1)
                nc.scalar.activation(low_part[:, b, :], lo_ps[b][:, :], ACT.Copy,
                                     scale=1.0 / LO).then_inc(S["low_done"], 1)

            copy_half(0, 0)
            copy_half(1, 1)
            low_out(0, 0)
            for n in range(2 * HT):
                act_e.wait_ge(S["w_tr"], n + 1)
                nc.scalar.activation(wT[:, n // HT, n % HT, :], (ea, eb)[n % 2][:, :], ACT.Copy)\
                    .then_inc(S["w_copied"], 1)
            copy_half(2, 0)
            low_out(1, 1)
            with act_e.Fori(3, T - 2, 2) as t:
                copy_half(t, 1)
                low_out(t - 1, 0)
                copy_half(t + 1, 0)
                low_out(t, 1)
            copy_half(T - 1, 1)
            low_out(T - 2, 0)
            low_out(T - 1, 1)

            act_e.wait_ge(S["nch_done"], 1)
            nch = act_e.value_load(nch_i[0:1, 0:1], min_val=1, max_val=CH)
            with act_e.Fori(0, nch) as c:
                for w, (ps, tr, cp) in enumerate(((ea, "subT_done", "subT_copied"), (eb, "objT_done", "objT_copied"))):
                    act_e.wait_ge(S[tr], c + 1)
                    nc.scalar.activation(gT[:, w, :, :].rearrange("p k e -> p (k e)"), ps[:, :], ACT.Copy)\
                        .then_inc(S[cp], 1)
            with act_e.Fori(0, nch) as c:
                act_e.wait_ge(S["dlt_done"], c + 1)
                nc.scalar.activation(pexp[:, :], dlt[:, :], ACT.Exp).then_inc(S["exp_done"], 1)
            act_e.wait_ge(S["m_final"], 1)
            nc.scalar.activation(e0[:, :, :], m_st[:, :, :], ACT.Exp, scale=-1.0).then_inc(S["row_exp_done"], 1)
            nc.scalar.activation(e1[:, :, :], m_st[:, :, :], ACT.Exp, scale=-1.0,
                                 bias=self_col[:, 0:1]).then_inc(S["row_exp_done"], 1)
            act_e.wait_ge(S["d1_done"], 1)
            with act_e.Fori(0, T) as t:
                nc.scalar.activation(xs[:, bass.ds(t, 1), :], xs[:, bass.ds(t, 1), :], ACT.Copy,
                                     scale=d1[:, bass.ds(t, 1)]).then_inc(S["scaled_done"], 1)
            with act_e.Fori(0, T // OG) as k:
                act_e.wait_ge(S["var_done"], k + 1)
                nc.scalar.activation(std[:, :], mv[:, :, 1], ACT.Sqrt)\
                    .then_inc(S["std_done"], 1)
                act_e.wait_ge(S["norm_ready"], k + 1)
                for i in range(OG // 2):
                    last = nc.scalar.activation(ax[:, bass.ds(k * OG + i, 1), :].rearrange("p a h -> p (a h)"), yb[:, i, :],
                                                ACT.Identity, scale=rstd[:, i:i + 1],
                                                bias=shift[:, i:i + 1])
                last.then_inc(S["act_norm_done"], 1)

        @block.tensor
        def _(pe):
            pe.wait_ge(S["const_dve"], 1)

            def transposes(t, b):
                pe.wait_ge(S["mask_done"], t + 1)
                for half, (done, copied) in enumerate((("tr0_done", "copy0_done"), ("tr1_done", "copy1_done"))):
                    if not isinstance(t, int) or t >= 1:
                        pe.wait_ge(S[copied], t)
                    for j in range(T // 2):
                        k = half * (T // 2) + j
                        last = nc.tensor.transpose(tp[half][:, j, :], mask[:, b, k * P:(k + 1) * P], ident16[:, :])
                    last.then_inc(S[done], 1)

            def products(t, b):
                pe.wait_ge(S["copy0_done"], t + 1)
                pe.wait_ge(S["copy1_done"], t + 1)
                if not isinstance(t, int) or t >= 2:
                    pe.wait_ge(S["ax_done"], t - 1)
                for j in range(T):
                    if isinstance(t, int) and t == 0 and j % XG == 0:
                        pe.wait_ge(S["xl_done"], j // XG + 1)
                    nc.tensor.matmul(hi_ps[b][:, :], maskT[:, b, j, :], xh[:, j, :], start=(j == 0), stop=(j == T - 1))
                    last = nc.tensor.matmul(lo_ps[b][:, :], maskT[:, b, j, :], xl[:, j, :],
                                            start=(j == 0), stop=(j == T - 1))
                last.then_inc(S["mm_done"], 1)

            transposes(0, 0)
            transposes(1, 1)
            products(0, 0)
            pe.wait_ge(S["w_in"], 32)
            for n in range(2 * HT):
                if n >= 2:
                    pe.wait_ge(S["w_copied"], n - 1)
                for o in range(HT):
                    last = nc.tensor.transpose((ea, eb)[n % 2][:, o * P:(o + 1) * P],
                                               wraw[:, n // HT, o, (n % HT) * P:(n % HT + 1) * P], ident[:, :])
                last.then_inc(S["w_tr"], 1)
            transposes(2, 0)
            products(1, 1)
            with pe.Fori(2, T - 2, 2) as t:
                transposes(t + 1, 1)
                products(t, 0)
                transposes(t + 2, 0)
                products(t + 1, 1)
            transposes(T - 1, 1)
            products(T - 2, 0)
            products(T - 1, 1)

            pe.wait_ge(S["act_sum_done"], 1)
            nc.tensor.matmul(ea[:, 0:1], after[0:EP, :], incl[0:EP, EC - 1:EC], start=True, stop=True)
            nc.tensor.matmul(ea[:, 1:2], ones[0:EP, :], incl[0:EP, EC - 1:EC], start=True, stop=True)\
                .then_inc(S["offs_done"], 1)
            pe.wait_ge(S["nch_done"], 1)
            nch = pe.value_load(nch_i[0:1, 0:1], min_val=1, max_val=CH)
            with pe.Fori(0, nch) as c:
                pe.wait_ge(S["onehot_done"], c + 1)
                for j in range(EC):
                    last = nc.tensor.matmul(ea[:, 0:3], onehot[0:EP, j, :], so16[0:EP, j, :],
                                            start=(j == 0), stop=(j == EC - 1))
                last.then_inc(S["compact_done"], 1)
                pe.wait_ge(S["kb_done"], c + 1)
                for w in range(2):
                    last = nc.tensor.transpose(eb[:, w * P:(w + 1) * P], kb[:, w, :], ident[:, :])
                last.then_inc(S["keyT_done"], 1)
                pe.wait_ge(S["sub_rows_in"], 16 * (c + 1))
                for k in range(HT):
                    last = nc.tensor.transpose(ea[:, k * P:(k + 1) * P], g[:, 0, k * P:(k + 1) * P], ident[:, :])
                last.then_inc(S["subT_done"], 1)
                pe.wait_ge(S["obj_rows_in"], 16 * (c + 1))
                pe.wait_ge(S["keyT_used"], c + 1)
                for k in range(HT):
                    last = nc.tensor.transpose(eb[:, k * P:(k + 1) * P], g[:, 1, k * P:(k + 1) * P], ident[:, :])
                last.then_inc(S["objT_done"], 1)
                for w, (ps, ready, done) in enumerate(((ea, "subT_copied", "q_done"), (eb, "objT_copied", "k_done"))):
                    pe.wait_ge(S[ready], c + 1)
                    for k in range(HT):
                        last = nc.tensor.matmul(ps[:, :], gT[:, w, k, :], wT[:, w, k, :],
                                                start=(k == 0), stop=(k == HT - 1))
                    last.then_inc(S[done], 1)
                pe.wait_ge(S["attB_done"], c + 1)
                for h in range(HEADS):
                    ps = (ea, eb)[h // 4]
                    last = nc.tensor.transpose(ps[:, (h % 4) * P:(h % 4 + 1) * P], attB[:, h, :], ident[:, :])
                last.then_inc(S["attT_done"], 1)
                pe.wait_ge(S["maxspread_done"], c + 1)
                nc.tensor.matmul(ea[:, 0:T * HEADS], hot_lo[:, :], spread8[:, :, :].rearrange("p t h -> p (t h)"),
                                 start=True, stop=True).then_inc(S["max_done"], 1)
            with pe.Fori(0, nch) as c:
                pe.wait_ge(S["hotlo_done"], c + 1)
                nc.tensor.transpose(eb[:, 0:P], hot_lo[:, :], ident[:, :]).then_inc(S["hotloT_done"], 1)
                pe.wait_ge(S["hotloT_copied"], c + 1)
                nc.tensor.matmul(ea[:, 0:T * HEADS], hot_loT[:, :], m_st[:, :, :].rearrange("p t h -> p (t h)"),
                                 start=True, stop=True).then_inc(S["mG_done"], 1)
                pe.wait_ge(S["zspread_done"], c + 1)
                nc.tensor.matmul(eb[:, 0:T * (HEADS + 1)], hot_lo[:, :], spread[:, :, :].rearrange("p t h -> p (t h)"),
                                 start=True, stop=True).then_inc(S["z_done"], 1)
            with pe.Fori(0, nch) as c:
                pe.wait_ge(S["hotlo3_done"], c + 1)
                nc.tensor.transpose(eb[:, 0:P], hot_lo[:, :], ident[:, :]).then_inc(S["hotloT3_done"], 1)
                pe.wait_ge(S["hotloT3_copied"], c + 1)
                nc.tensor.matmul(ea[:, 0:T * (HEADS + 1)], hot_loT[:, :],
                                 rz_st[:, :, :].rearrange("p t h -> p (t h)"),
                                 start=True, stop=True).then_inc(S["rzG_done"], 1)
                pe.wait_ge(S["wL_done"], c + 1)
                pe.wait_ge(S["obj2_rows_in"], 16 * (c + 1))
                for t in range(T):
                    if t >= 2:
                        pe.wait_ge(S["edge_added"], c * T + t - 1)
                    nc.tensor.matmul((ea, eb)[t % 2][:, :], wL[:, t, :], g[:, 1, :], start=True, stop=True)\
                        .then_inc(S["edge_mm_done"], 1)

        @block.vector
        def _(dve):
            v = nc.vector
            setup = Chain(dve, S["dve_setup"])
            dve.wait_ge(S["const_pool"], 8)
            v.tensor_copy(ident16[:, :], ident[:, :]).then_inc(S["const_dve"], 1)
            v.tensor_copy(iota16[:, :], iota_f[:, :])
            v.memset(self_col[:, :], SELF).then_inc(S["dve_norm_done"], 1)
            v.memset(m_st[:, :, :], SELF)
            v.memset(z_st[:, :, :], 0.0)
            v.memset(zeros80[:, :], 0.0)
            v.memset(own_g[:, :], -1)
            setup(v.memset(so16[:, :, :], 1.0))
            dve.wait_ge(S["pairs_in"], 16)
            setup(v.tensor_copy(prf[0:EP], pr[0:EP]))
            v.tensor_copy(so16[0:EP, :, 0:2], prf[0:EP])
            setup(v.scalar_tensor_tensor(out=keyf[0:EP], in0=prf[0:EP, :, 0], scalar=float(N), in1=prf[0:EP, :, 1],
                                         op0=ALU.mult, op1=ALU.add))
            v.tensor_copy(key_i[0:EP], keyf[0:EP]).then_inc(S["keys_done"], 1)

            def make_mask(t, b, link):
                if isinstance(t, int):
                    dve.wait_ge(S[f"adj_in{b}"], 16 * (t // 2 + 1))
                else:
                    dve.wait_ge(S[f"adj_in{b}"], 8 * (t - b) + 16)
                diag = adjf[:, b, t * P:(t + 1) * P] if isinstance(t, int) else adjf[:, b, bass.ds(t * P, P)]
                link(v.tensor_tensor(diag, diag, offdiag[:, :], ALU.mult))
                if not isinstance(t, int) or t >= 2:
                    dve.wait_ge(S["tr1_done"], t - 1)
                count = rowsum[:, t:t + 1] if isinstance(t, int) else rowsum[:, bass.ds(t, 1)]
                v.tensor_scalar(mask[:, b, :], adjf[:, b, :], 1.0, 0.0, ALU.is_equal, ALU.add, accum_out=count)\
                    .then_inc(S["mask_done"], 1)

            def copy_half(t, b):
                dve.wait_ge(S["tr1_done"], t + 1)
                if not isinstance(t, int) or t >= 2:
                    dve.wait_ge(S["mm_done"], t - 1)
                v.tensor_copy(maskT[:, b, T // 2:T, :], tp[1][:, :, :]).then_inc(S["copy1_done"], 1)

            def sum_halves(t, b):
                dve.wait_ge(S["low_done"], t + 1)
                dst = ax[:, t:t + 1, :] if isinstance(t, int) else ax[:, bass.ds(t, 1), :]
                v.tensor_tensor(dst.rearrange("p a h -> p (a h)"), hi_ps[b][:, :], low_part[:, b, :], ALU.add)\
                    .then_inc(S["ax_done"], 1)

            tile = Chain(dve, S["dve_tile"])
            make_mask(0, 0, tile)
            for i in range(T // XG):
                piece = slice(i * XG, (i + 1) * XG)
                dve.wait_ge(S["xh_done"], i + 1)
                if i >= 2:
                    dve.wait_ge(S["xl_done"], i - 1)
                v.tensor_tensor(diff[:, i % 2, :], xs[:, piece, :].rearrange("p a b -> p (a b)"),
                                xh[:, piece, :].rearrange("p a b -> p (a b)"), ALU.subtract).then_inc(S["diff_done"], 1)
            make_mask(1, 1, tile)
            copy_half(0, 0)
            make_mask(2, 0, tile)
            copy_half(1, 1)
            dve.wait_ge(S["w_copied"], 2 * HT)
            sum_halves(0, 0)
            make_mask(3, 1, tile)
            copy_half(2, 0)
            sum_halves(1, 1)
            with dve.Fori(3, T - 2, 2) as t:
                make_mask(t + 1, 0, Chain(dve, S["dve_tile"], t + 1))
                copy_half(t, 1)
                sum_halves(t - 1, 0)
                make_mask(t + 2, 1, Chain(dve, S["dve_tile"], t + 2))
                copy_half(t + 1, 0)
                sum_halves(t, 1)
            copy_half(T - 1, 1)
            sum_halves(T - 2, 0)
            sum_halves(T - 1, 1)

            flags = Chain(dve, S["dve_flags"])
            flags(v.tensor_tensor(act[0:EP], prf[0:EP, :, 0], prf[0:EP, :, 1], ALU.not_equal))
            dve.wait_ge(S["adjv_in"], 16 * EC)
            flags(v.scalar_tensor_tensor(out=act[0:EP], in0=adjv[0:EP], scalar=1.0, in1=act[0:EP],
                                         op0=ALU.is_equal, op1=ALU.mult))
            v.tensor_tensor_scan(out=incl[0:EP], data0=act[0:EP], data1=zeros80[0:EP], initial=0.0,
                                 op0=ALU.add, op1=ALU.add).then_inc(S["act_sum_done"], 1)
            dve.wait_ge(S["offs_done"], 1)
            flags(v.tensor_copy(offs[:, :], ea[:, 0:2]))
            flags(v.tensor_scalar(chunk_tmp[:, :], chunk_lo[:, :], offs[:, 1:2], 0.0, ALU.is_lt, ALU.add,
                                  accum_out=nch_f[:, 0:1]))
            flags(v.tensor_scalar(nch_f[:, 1:2], nch_f[:, 0:1], 1.0, None, ALU.max))
            v.tensor_copy(nch_i[:, :], nch_f[:, 1:2]).then_inc(S["nch_done"], 1)
            flags(v.tensor_scalar(slot[0:EP], incl[0:EP], offs[0:EP, 0:1], None, ALU.add))
            flags(v.tensor_tensor(slot[0:EP], slot[0:EP], act[0:EP], ALU.mult))
            flags(v.tensor_scalar(slot[0:EP], slot[0:EP], -1.0, None, ALU.add))
            flags(v.tensor_copy(slotv, slot0[:, :]))
            dve.wait_ge(S["nch_done"], 1)
            nch = dve.value_load(nch_i[0:1, 0:1], min_val=1, max_val=CH)

            def column(c, i):
                return col_all[:, bass.ds(c, 1), i:i + 1].rearrange("p a b -> p (a b)")

            STEPS1 = 28
            with dve.Fori(0, nch) as c:
                step = Chain(dve, S["dve_scan"], c * STEPS1)
                step(v.tensor_scalar(slot16[0:EP], slot[0:EP], -1.0, float(P), ALU.max, ALU.min))
                v.tensor_tensor(onehot[0:EP], iota16[0:EP].unsqueeze(1).to_broadcast([EP, EC, P]),
                                slot16[0:EP].unsqueeze(2).to_broadcast([EP, EC, P]), ALU.is_equal)\
                    .then_inc(S["onehot_done"], 1)
                step(v.tensor_scalar(slot[0:EP], slot[0:EP], -float(P), None, ALU.add))
                dve.wait_ge(S["compact_done"], c + 1)
                step(v.tensor_copy(se[:, :], ea[:, 0:3]))
                step(v.tensor_copy(si[:, :], se[:, 0:2]))
                v.scalar_tensor_tensor(out=keyv, in0=se[:, 0:1], scalar=float(N), in1=se[:, 1:2],
                                       op0=ALU.mult, op1=ALU.add).then_inc(S["idx_done"], 1)
                v.tensor_scalar(split_i[:, 0:1], si[:, 0:1], 7, None, ALU.arith_shift_right)
                step(v.tensor_scalar(split_i[:, 1:2], si[:, 0:1], P - 1, None, ALU.bitwise_and))
                step(v.tensor_copy(split_f[:, :], split_i[:, :]))
                valid = se[:, 2:3]
                v.tensor_scalar(keyv, keyv, 1.0, valid, ALU.add, ALU.mult)
                v.tensor_scalar(subv, se[:, 0:1], 1.0, valid, ALU.add, ALU.mult)
                step(v.tensor_scalar(hiv, split_f[:, 0:1], 1.0, valid, ALU.add, ALU.mult))
                step(v.tensor_scalar(cols[:, 0:2], cols[:, 0:2], -1.0, None, ALU.add))
                step(v.tensor_scalar(hiv, hiv, -1.0, None, ALU.add))
                v.tensor_copy(column(c, 0), hiv)
                v.tensor_copy(column(c, 1), split_f[:, 1:2])
                v.tensor_copy(column(c, 2), se[:, 1:2])
                v.tensor_copy(column(c, 3), valid)
                v.tensor_copy(kb[:, :, :], cols[:, 0:2].unsqueeze(2).to_broadcast([P, 2, P])).then_inc(S["kb_done"], 1)
                v.tensor_scalar(hot_hi[:, :], iota_f[:, 0:T], hiv, None, ALU.is_equal)
                step(v.tensor_scalar(hot_lo[:, :], iota_f[:, :], split_f[:, 1:2], None, ALU.is_equal))
                dve.wait_ge(S["keyT_done"], c + 1)
                step(v.scalar_tensor_tensor(out=junk[:, :], in0=eb[:, 0:P], scalar=keyv, in1=before[:, :],
                                            op0=ALU.is_equal, op1=ALU.mult, accum_out=dup))
                v.tensor_scalar(same[:, :], eb[:, P:2 * P], subv, None, ALU.is_equal).then_inc(S["keyT_used"], 1)
                dve.wait_ge(S["keyT_used"], c + 1)
                step(v.scalar_tensor_tensor(out=junk[:, :], in0=same[:, :], scalar=1.0, in1=before[:, :],
                                            op0=ALU.mult, op1=ALU.mult, accum_out=cnt))
                step(v.tensor_scalar(uniq, dup, 0.0, valid, ALU.is_equal, ALU.mult))
                step(v.tensor_scalar(rep, cnt, 0.0, valid, ALU.is_equal, ALU.mult))
                step(v.tensor_scalar(k2, uniq, -float(2 * N * N), float(2 * N * N), ALU.mult, ALU.add))
                step(v.tensor_tensor(skey_f, keyv, k2, ALU.add))
                step(v.tensor_scalar(skey_f, skey_f, -1.0, None, ALU.max))
                v.tensor_copy(slot_i[:, :], slotv)
                v.tensor_copy(skey_i[:, :], skey_f).then_inc(S["skey_done"], 1)
                for w, done in enumerate(("q_done", "k_done")):
                    dve.wait_ge(S[done], c + 1)
                    step(v.tensor_tensor(qk[:, w, :], (ea, eb)[w][:, :], bias[:, w, :], ALU.add))
                step(v.tensor_tensor(qk[:, 2, :], qk[:, 0, :], qk[:, 1, :], ALU.mult))
                step(v.tensor_reduce(att1[:, :], qk[:, 2, :].rearrange("p (h d) -> p h d", h=HEADS), AX.X, ALU.add))
                step(v.tensor_scalar(att1[:, :], att1[:, :], DK ** -0.5, valid, ALU.mult, ALU.mult))
                v.tensor_copy(att_all[:, bass.ds(c, 1), :].rearrange("p a h -> p (a h)"), att1[:, :])
                v.tensor_copy(attB[:, :, :], att1[:, :].unsqueeze(2).to_broadcast([P, HEADS, P]))\
                    .then_inc(S["attB_done"], 1)
                dve.wait_ge(S["attT_done"], c + 1)
                for i, ps in enumerate((ea, eb)):
                    out_ = attM[:, 4 * i:4 * i + 4, :]
                    step(v.tensor_tensor(out_, ps[:, :].rearrange("p (h e) -> p h e", h=4),
                                         same[:, :].unsqueeze(1).to_broadcast([P, 4, P]), ALU.mult))
                step(v.tensor_reduce(seg[:, :], attM[:, :, :], AX.X, ALU.max))
                step(v.tensor_scalar(seg[:, :], seg[:, :], rep, None, ALU.mult))
                v.tensor_tensor(spread8[:, :, :], hot_hi[:, :].unsqueeze(2).to_broadcast([P, T, HEADS]),
                                seg[:, :].unsqueeze(1).to_broadcast([P, T, HEADS]), ALU.mult)\
                    .then_inc(S["maxspread_done"], 1)
                dve.wait_ge(S["max_done"], c + 1)
                step(v.tensor_tensor(m_st[:, :, :], m_st[:, :, :],
                                     ea[:, 0:T * HEADS].rearrange("p (t h) -> p t h", h=HEADS), ALU.max))
                dve.wait_ge(S["owner_out"], 16 * (c + 1))
                step(v.tensor_scalar(slotv, slotv, float(P), None, ALU.add))
                assert step.n == STEPS1, step.n
            v.tensor_copy(junk[:, 0:1], self_col[:, :]).then_inc(S["m_final"], 1)

            again = Chain(dve, S["dve_exp"])
            again(v.tensor_copy(slotv, slot0[:, :]))
            STEPS2 = 12
            with dve.Fori(0, nch) as c:
                step = Chain(dve, S["dve_exp"], c * STEPS2 + 1)
                v.tensor_scalar(hot_hi[:, :], iota_f[:, 0:T], column(c, 0), None, ALU.is_equal)
                v.tensor_scalar(hot_lo[:, :], iota_f[:, :], column(c, 1), None, ALU.is_equal)\
                    .then_inc(S["hotlo_done"], 1)
                step(v.scalar_tensor_tensor(out=subv, in0=column(c, 0), scalar=float(P), in1=column(c, 1),
                                            op0=ALU.mult, op1=ALU.add))
                step(v.scalar_tensor_tensor(out=keyv, in0=subv, scalar=float(N), in1=column(c, 2),
                                            op0=ALU.mult, op1=ALU.add))
                step(v.tensor_scalar(k2, column(c, 3), -float(2 * N * N), float(2 * N * N), ALU.mult, ALU.add))
                step(v.tensor_tensor(skey_f, keyv, k2, ALU.add))
                v.tensor_copy(skey_i[:, :], skey_f).then_inc(S["key2_done"], 1)
                dve.wait_ge(S["hotloT_done"], c + 1)
                v.tensor_copy(hot_loT[:, :], eb[:, 0:P]).then_inc(S["hotloT_copied"], 1)
                dve.wait_ge(S["mG_done"], c + 1)
                step(v.tensor_tensor(spread8[:, :, :], ea[:, 0:T * HEADS].rearrange("p (t h) -> p t h", h=HEADS),
                                     hot_hi[:, :].unsqueeze(2).to_broadcast([P, T, HEADS]), ALU.mult))
                step(v.tensor_reduce(seg[:, :], spread8[:, :, :].rearrange("p t h -> p h t"), AX.X, ALU.add))
                v.tensor_tensor(dlt[:, :], att_all[:, bass.ds(c, 1), :].rearrange("p a h -> p (a h)"), seg[:, :],
                                ALU.subtract).then_inc(S["dlt_done"], 1)
                dve.wait_ge(S["owner_in"], 16 * (c + 1))
                step(v.tensor_copy(own_f[:, :], own_g[:, :]))
                step(v.tensor_tensor(owned, own_f[:, :], slotv, ALU.is_equal))
                step(v.tensor_tensor(owned, owned, column(c, 3), ALU.mult))
                step(v.tensor_scalar(slotv, slotv, float(P), None, ALU.add))
                v.tensor_copy(column(c, 5), owned)
                v.tensor_copy(e9[:, HEADS:HEADS + 1], owned)
                dve.wait_ge(S["exp_done"], c + 1)
                step(v.tensor_scalar(e9[:, 0:HEADS], pexp[:, :], owned, None, ALU.mult))
                v.tensor_copy(p_all[:, bass.ds(c, 1), :].rearrange("p a h -> p (a h)"), e9[:, 0:HEADS])
                v.tensor_tensor(spread[:, :, :], hot_hi[:, :].unsqueeze(2).to_broadcast([P, T, HEADS + 1]),
                                e9[:, :].unsqueeze(1).to_broadcast([P, T, HEADS + 1]), ALU.mult)\
                    .then_inc(S["zspread_done"], 1)
                dve.wait_ge(S["z_done"], c + 1)
                step(v.tensor_tensor(z_st[:, :, :], z_st[:, :, :],
                                     eb[:, 0:T * (HEADS + 1)].rearrange("p (t h) -> p t h", h=HEADS + 1), ALU.add))
                assert step.n == STEPS2, step.n

            rows = Chain(dve, S["dve_rows"])
            rows(v.tensor_tensor(n0[:, :], rowsum[:, :], z_st[:, :, HEADS], ALU.subtract))
            dve.wait_ge(S["row_exp_done"], 2)
            rows(v.tensor_tensor(rt[:, :, :], e0[:, :, :], n0[:, :].unsqueeze(2).to_broadcast([P, T, HEADS]), ALU.mult))
            rows(v.tensor_tensor(rt[:, :, :], rt[:, :, :], e1[:, :, :], ALU.add))
            rows(v.tensor_tensor(rt[:, :, :], rt[:, :, :], z_st[:, :, 0:HEADS], ALU.add))
            rows(v.reciprocal(rt[:, :, :], rt[:, :, :]))
            rows(v.tensor_scalar(rz_st[:, :, 0:HEADS], rt[:, :, :], 1.0 / HEADS, None, ALU.mult))
            rows(v.tensor_tensor(rt[:, :, :], rz_st[:, :, 0:HEADS], e1[:, :, :], ALU.mult))
            rows(v.tensor_reduce(d1[:, :], rt[:, :, :], AX.X, ALU.add))
            v.tensor_scalar(d1[:, :], d1[:, :], 1.0, None, ALU.add).then_inc(S["d1_done"], 1)
            rows(v.tensor_tensor(e0[:, :, :], rz_st[:, :, 0:HEADS], e0[:, :, :], ALU.mult))
            rows(v.tensor_reduce(rz_st[:, :, HEADS], e0[:, :, :], AX.X, ALU.add))
            dve.wait_ge(S["scaled_done"], T)

            STEPS3 = 6
            with dve.Fori(0, nch) as c:
                step = Chain(dve, S["dve_edges"], c * STEPS3)
                v.tensor_copy(obj_i[:, :], column(c, 2)).then_inc(S["obj2_done"], 1)
                v.tensor_scalar(hot_hi[:, :], iota_f[:, 0:T], column(c, 0), None, ALU.is_equal)
                v.tensor_scalar(hot_lo[:, :], iota_f[:, :], column(c, 1), None, ALU.is_equal)\
                    .then_inc(S["hotlo3_done"], 1)
                dve.wait_ge(S["hotloT3_done"], c + 1)
                v.tensor_copy(hot_loT[:, :], eb[:, 0:P]).then_inc(S["hotloT3_copied"], 1)
                dve.wait_ge(S["rzG_done"], c + 1)
                step(v.tensor_tensor(spread[:, :, :], ea[:, 0:T * (HEADS + 1)].rearrange("p (t h) -> p t h", h=HEADS + 1),
                                     hot_hi[:, :].unsqueeze(2).to_broadcast([P, T, HEADS + 1]), ALU.mult))
                step(v.tensor_reduce(e9[:, :], spread[:, :, :].rearrange("p t h -> p h t"), AX.X, ALU.add))
                step(v.tensor_tensor(dlt[:, :], p_all[:, bass.ds(c, 1), :].rearrange("p a h -> p (a h)"),
                                     e9[:, 0:HEADS], ALU.mult))
                step(v.tensor_reduce(wcol, dlt[:, :], AX.X, ALU.add))
                step(v.tensor_scalar(wcol, wcol, e9[:, HEADS:HEADS + 1], column(c, 5), ALU.subtract, ALU.mult))
                step(v.tensor_scalar(hot_hi[:, :], hot_hi[:, :], wcol, None, ALU.mult))
                v.tensor_tensor(wL[:, :, :], hot_lo[:, :].unsqueeze(1).to_broadcast([P, T, P]),
                                hot_hi[:, :].unsqueeze(2).to_broadcast([P, T, P]), ALU.mult).then_inc(S["wL_done"], 1)
                for t in range(T):
                    dve.wait_ge(S["edge_mm_done"], c * T + t + 1)
                    v.tensor_tensor(xs[:, t, :], xs[:, t, :], (ea, eb)[t % 2][:, :], ALU.add)\
                        .then_inc(S["edge_added"], 1)
                dve.wait_ge(S["edge_added"], c * T + T)
                assert step.n == STEPS3, step.n

            NSTEPS = 5
            with dve.Fori(0, T // OG) as k:
                step = Chain(dve, S["dve_norm"], k * NSTEPS)
                dve.wait_ge(S["act_norm_done"], k + 1)
                dve.wait_ge(S["dve_norm_done"], k + 1)
                for i in range(OG):
                    t1 = bass.ds(k * OG + i, 1)
                    ins = v.scalar_tensor_tensor(out=yb[:, i, :], in0=ax[:, t1, :].rearrange("p a h -> p (a h)"),
                                                 scalar=rz_st[:, t1, HEADS:HEADS + 1].rearrange("p a b -> p (a b)"),
                                                 in1=xs[:, t1, :].rearrange("p a h -> p (a h)"),
                                                 op0=ALU.mult, op1=ALU.add)
                step(ins)
                for i in range(OG):
                    ins = v.bn_stats(stats[:, i, :], yb[:, i, :])
                step(ins)
                v.memset(junk[:, 0:1], 0.0)
                for i in range(OG):
                    ins = v.bn_aggr(mv[:, i, :], stats[:, i, :])
                step(ins)
                v.tensor_scalar(mv[:, :, 1], mv[:, :, 1], EPS, None, ALU.add).then_inc(S["var_done"], 1)
                dve.wait_ge(S["std_done"], k + 1)
                step(v.reciprocal(rstd[:, :], std[:, :]))
                step(v.tensor_tensor(shift[:, :], mv[:, :, 0], rstd[:, :], ALU.mult))
                v.tensor_scalar(shift[:, :], shift[:, :], -1.0, None, ALU.mult).then_inc(S["norm_ready"], 1)
                dve.wait_ge(S["norm_ready"], k + 1)
                for i in range(OG // 2, OG):
                    t1 = bass.ds(k * OG + i, 1)
                    row = ax[:, t1, :].rearrange("p a h -> p (a h)")
                    last = v.tensor_scalar(row, yb[:, i, :], rstd[:, i:i + 1], shift[:, i:i + 1], ALU.mult, ALU.add)
                last.then_inc(S["dve_norm_done"], 1)
                assert step.n == NSTEPS, step.n


_INS = ['x', 'adj', 'L0_gnn_rel_pair_index', 'L0_gnn_Wq', 'L0_gnn_bq', 'L0_gnn_Wk', 'L0_gnn_bk']
_OUTS = [((2048, 512), 'float32')]


def kernel(**inputs):
    import numpy as _np
    import concourse.bacc as _bacc
    from concourse import mybir as _mybir
    from concourse.bass_utils import run_bass_kernel_spmd as _run

    nc = _bacc.Bacc("TRN2", target_bir_lowering=False, num_devices=1)
    arrays, args = {}, []
    for name in _INS:
        a = _np.ascontiguousarray(inputs[name])
        arrays[f"in_{name}_dram"] = a
        args.append(nc.dram_tensor(f"in_{name}_dram", a.shape, _mybir.dt.from_np(a.dtype), kind="ExternalInput").ap())
    for i, (shape, dtype) in enumerate(_OUTS):
        dt = _mybir.dt.from_np(_np.dtype(dtype))
        args.append(nc.dram_tensor(f"out_{i}_dram", shape, dt, kind="ExternalOutput").ap())
    gnn_attention_layernorm_kernel(nc, *args)
    r = _run(nc, [arrays], core_ids=[0])
    got = tuple(r.results[0][f"out_{i}_dram"] for i in range(len(_OUTS)))
    return got[0]
```

```python
import concourse.bass as bass
from concourse import mybir
from contextlib import ExitStack


class Chain:

    def __init__(self, engine, sem, base=0):
        self.engine, self.sem, self.base, self.n = engine, sem, base, 0

    def __call__(self, ins):
        self.n += 1
        ins.then_inc(self.sem, 1)
        self.engine.wait_ge(self.sem, self.base + self.n)


def gnn_attention_layernorm_kernel(
    nc: bass.Bass,
    x: bass.AP,
    adj: bass.AP,
    pairs: bass.AP,
    Wq: bass.AP,
    bq: bass.AP,
    Wk: bass.AP,
    bk: bass.AP,
    out: bass.AP,
):
    fp32, fp16, i32 = mybir.dt.float32, mybir.dt.float16, mybir.dt.int32
    ALU = mybir.AluOpType
    ACT = mybir.ActivationFunctionType
    AX = mybir.AxisListType

    P = 128
    N, H = x.shape
    T = N // P
    HT = H // P
    HEADS = 8
    DK = H // HEADS
    E = pairs.shape[0]
    EC = 80
    EP = E // EC
    assert EP * EC == E and EP <= P
    CH = -(-E // P)
    SELF = 1e-7
    EPS = 1e-5
    LO = 2048.0
    PAST = float(2 * N * N)
    XG = 2
    XP = T // XG
    OG = 2
    MB = 4
    Q = 4
    TQ = T // Q
    CG = 16
    NG = EC // CG
    LOOP = (2, 10)
    assert EC % CG == 0 and (LOOP[1] - LOOP[0]) % MB == 0 and LOOP[0] == OG

    owner = nc.dram_tensor("owner", [N * N, 1], i32, kind="Internal").ap()
    ax_dram = nc.dram_tensor("ax_dram", [N, H], fp32, kind="Internal").ap()
    count_dram = nc.dram_tensor("count_dram", [N, 1], fp32, kind="Internal").ap()
    adj_flat = adj.rearrange("a (b o) -> (a b) o", o=1)
    x_tiles = x.rearrange("(t p) h -> p t h", p=P)
    out_tiles = out.rearrange("(t p) h -> p t h", p=P)
    ax_tiles = ax_dram.rearrange("(t p) h -> p t h", p=P)

    ctx = ExitStack()
    with ctx:
        def sb(name, shape, dt=fp32):
            return ctx.enter_context(nc.sbuf_tensor(name, shape, dt))

        def pb(name, shape, dt=fp32):
            return ctx.enter_context(nc.psum_tensor(name, shape, dt))

        ident = sb("ident", [P, P])
        ident16 = sb("ident16", [P, P], fp16)
        offdiag = sb("offdiag", [P, P])
        before = sb("before", [P, P])
        after = sb("after", [P, P])
        ones = sb("ones", [P, P])
        iota_f = sb("iota_f", [P, P])
        iota16 = sb("iota16", [P, P], fp16)
        slot0 = sb("slot0", [P, 1])
        chunk_lo = sb("chunk_lo", [P, CH])
        self_col = sb("self_col", [P, 1])
        plain_e0 = sb("plain_e0", [P, 1])
        xs = sb("xs", [P, T, H])
        xh = sb("xh", [P, T, H], fp16)
        xl = sb("xl", [P, T, H], fp16)
        adjf = sb("adjf", [P, 2, N])
        mask = sb("mask", [P, MB, N], fp16)
        maskT = sb("maskT", [P, 2, T, P], fp16)
        low_part = sb("low_part", [P, 2, H])
        ax = sb("ax", [P, T, H])
        wraw = ax[:, 0:2 * HT, :].rearrange("p (w o) i -> p w o i", w=2)
        count = sb("count", [P, T])
        wT = sb("wT", [P, 2, HT, H])
        bias = sb("bias", [P, 2, H])
        pr = sb("pr", [P, EC, 2], i32)
        prf = sb("prf", [P, EC, 2])
        so16 = sb("so16", [P, EC, 3], fp16)
        keyf = sb("keyf", [P, EC])
        key_i = sb("key_i", [P, EC], i32)
        adjv = sb("adjv", [P, EC])
        act = sb("act", [P, EC])
        incl = sb("incl", [P, EC])
        zeros = sb("zeros", [P, EC])
        slot = sb("slot", [P, EC])
        slot16 = sb("slot16", [P, EC], fp16)
        offs = sb("offs", [P, 2])
        nch_f = sb("nch_f", [P, 2])
        nch_i = sb("nch_i", [P, 1], i32)
        chunk_tmp = sb("chunk_tmp", [P, CH])
        area = sb("area", [P, 2560])
        diff = area[:, 0:2 * XG * H].rearrange("p (b n) -> p b n", b=2)
        onehot = area[:, 0:CG * P].bitcast(fp16).rearrange("p (b c s) -> p b c s", b=2, s=P)
        gT = area[:, 0:2 * HT * P].rearrange("p (w k e) -> p w k e", w=2, k=HT)
        attM = area[:, 0:HEADS * P].rearrange("p (h e) -> p h e", h=HEADS)
        qk = area[:, 1024:1024 + 3 * H].rearrange("p (w h) -> p w h", w=3)
        attB = area[:, 1024:1024 + HEADS * P].rearrange("p (h e) -> p h e", h=HEADS)
        wL = area[:, 0:T * P].rearrange("p (t e) -> p t e", t=T)
        g = sb("g", [P, 2, H])
        axg = g[:, 1, :]
        se = sb("se", [P, 3])
        si = sb("si", [P, 2], i32)
        split_i = sb("split_i", [P, 2], i32)
        split_f = sb("split_f", [P, 2])
        cols = sb("cols", [P, 24])
        keyv, subv, dup, cnt, rep, uniq = (cols[:, i:i + 1] for i in range(6))
        hiv, lov, objv, slotv, wcol, owned = (cols[:, i:i + 1] for i in range(6, 12))
        skey_f, k2, place_f, row_f, n_edge, c_edge = (cols[:, i:i + 1] for i in range(12, 18))
        d_edge, var1, shift1, rstd1 = (cols[:, i:i + 1] for i in range(18, 22))
        skey_i = sb("skey_i", [P, 1], i32)
        slot_i = sb("slot_i", [P, 1], i32)
        obj_i = sb("obj_i", [P, 1], i32)
        place_i = sb("place_i", [P, 1], i32)
        row_i = sb("row_i", [P, 1], i32)
        count_g = sb("count_g", [P, 1])
        own_g = sb("own_g", [P, 1], i32)
        own_f = sb("own_f", [P, 1])
        kb = sb("kb", [P, 2, P])
        same = sb("same", [P, P])
        sameW = kb[:, 0, :]
        junk = sb("junk", [P, P])
        att1 = sb("att1", [P, HEADS])
        seg = sb("seg", [P, HEADS])
        hot_lo = sb("hot_lo", [P, P])
        hot_hi = sb("hot_hi", [P, T])
        hot_loT = sb("hot_loT", [P, P])
        spread = sb("spread", [P, T, HEADS + 1])
        spread8 = sb("spread8", [P, T, HEADS])
        e9 = sb("e9", [P, HEADS + 1])
        dlt = sb("dlt", [P, HEADS])
        pexp = sb("pexp", [P, HEADS])
        x0 = sb("x0", [P, HEADS])
        x1 = sb("x1", [P, HEADS])
        xz = sb("xz", [P, HEADS])
        st1 = sb("st1", [P, 6])
        mv1 = sb("mv1", [P, 2])
        att_all = sb("att_all", [P, CH, HEADS])
        p_all = sb("p_all", [P, CH, HEADS])
        col_all = sb("col_all", [P, CH, 6])
        m_st = sb("m_st", [P, T, HEADS])
        z_st = sb("z_st", [P, T, HEADS + 1])
        rz_st = sb("rz_st", [P, T, HEADS + 1])
        e0 = sb("e0", [P, T, HEADS])
        e1 = sb("e1", [P, T, HEADS])
        rt = sb("rt", [P, T, HEADS])
        n0 = sb("n0", [P, T])
        d1 = sb("d1", [P, T])
        zc = sb("zc", [P, OG])
        cc = sb("cc", [P, OG])
        dc = sb("dc", [P, OG])
        yb = sb("yb", [P, 2, OG, H])
        stats = sb("stats", [P, OG, 6])
        mv = sb("mv", [P, OG, 2])
        std = sb("std", [P, OG])
        rstd = sb("rstd", [P, OG])
        shift = sb("shift", [P, OG])

        tp = [pb(f"tp{i}", [P, TQ, P]) for i in range(2)]
        hi_ps = [pb(f"hi_ps{i}", [P, H]) for i in range(2)]
        lo_ps = [pb(f"lo_ps{i}", [P, H]) for i in range(2)]
        ea = pb("ea", [P, H])
        eb = pb("eb", [P, H])

        names = """pairs_in adj_in0 adj_in1 w_in bias_in const_pool const_dve plain_done
            xh_done diff_done xl_done w_tr w_copied keys_done adjv_in
            mask_done tr_done copy_done mm_done low_done ax_done cd_done t1_done var_done std_done norm_ready
            norm_done yb_free out_done ax_out count_out
            act_sum_done offs_done nch_done
            f_onehot_done f_compact_part f_idx_done f_sub_rows_in f_obj_rows_in f_kb_done f_keyT_done f_keyT_used
            f_subT_done f_subT_copied f_objT_done f_objT_copied f_q_done f_k_done f_attB_done f_attT_done
            f_place_done f_count_in f_seg_done f_exp_done f_e9_done f_z_done f_sameW_done f_edges_done f_pre_done
            f_ax_in f_var_done f_std_done f_row_done f_row_out
            onehot_done compact_part idx_done sub_rows_in obj_rows_in kb_done keyT_done keyT_used skey_done
            owner_out subT_done subT_copied objT_done objT_copied q_done k_done attB_done attT_done
            maxspread_done max_done
            hotlo_done hotloT_done hotloT_copied mG_done dlt_done exp_done zspread_done z_done key2_done owner_in
            m_final row_exp_done d1_done scaled_done
            obj2_done obj2_rows_in rzG_done wL_done edge_mm_done edge_added hotlo3_done hotloT3_done hotloT3_copied
            g_var_done g_std_done g_norm_ready g_act_norm_done g_dve_norm_done g_out_done
            dve_setup dve_tile dve_plain dve_flags dve_fast dve_scan dve_max dve_exp dve_rows dve_edges dve_norm
            """.split() + [f"x_in{i}" for i in range(XP)]
        S = {n: ctx.enter_context(nc.semaphore(n)) for n in names}

        def tile_of(tensor, t):
            at = tensor[:, t:t + 1, :] if isinstance(t, int) else tensor[:, bass.ds(t, 1), :]
            return at.rearrange("p a h -> p (a h)")

        def flat(ap):
            return ap.rearrange("p a b -> p (a b)")

        def wide(ap, n):
            return ap.unsqueeze(2).to_broadcast([ap.shape[0], ap.shape[1], n])

        def times(ap, n):
            return ap.unsqueeze(1).to_broadcast([ap.shape[0], n, ap.shape[1]])

        block = ctx.enter_context(nc.Block())

        @block.sync
        def _(sp):
            def load_adj(t, b):
                if not isinstance(t, int) or t >= 2:
                    sp.wait_ge(S["mask_done"], t - 1)
                rows = adj[t * P:(t + 1) * P, :] if isinstance(t, int) else adj[bass.ds(t * P, P), :]
                sp.dma_start(adjf[:, b, :], rows).then_inc(S[f"adj_in{b}"], 16)

            def load_x(i):
                sp.dma_start(xs[:, i * XG:(i + 1) * XG, :],
                             x_tiles[:, i * XG:(i + 1) * XG, :]).then_inc(S[f"x_in{i}"], 16)

            def store_ax(t, n):
                sp.wait_ge(S["ax_done"], t + n + 2)
                at = slice(t, t + n) if isinstance(t, int) else bass.ds(t, n)
                sp.dma_start(ax_tiles[:, at, :], ax[:, at, :]).then_inc(S["ax_out"], 16)

            def store_pair(t, pb_):
                number = t // OG if isinstance(t, int) else t // OG
                sp.wait_ge(S["norm_done"], number + 2)
                at = slice(t, t + OG) if isinstance(t, int) else bass.ds(t, OG)
                sp.dma_start(out_tiles[:, at, :], yb[:, pb_, :, :]).then_inc(S["out_done"], 16)
                sp.wait_ge(S["out_done"], 16 * (number + 1))
                sp.nop().then_inc(S["yb_free"], 1)

            sp.dma_start(pr[0:EP], pairs.rearrange("(p c) w -> p c w", p=EP)).then_inc(S["pairs_in"], 16)
            load_x(0)
            load_x(1)
            load_adj(0, 0)
            for i in range(2, XP):
                load_x(i)
            load_adj(1, 1)
            for w, src in enumerate((Wq, Wk)):
                sp.dma_start(wraw[:, w, :, :], src.rearrange("(o p) i -> p o i", p=P)).then_inc(S["w_in"], 16)
            for w, src in enumerate((bq, bk)):
                sp.dma_start(bias[:, w, :], src.partition_broadcast(P)).then_inc(S["bias_in"], 16)
            for t in range(2, LOOP[0] + MB + 2):
                load_adj(t, t % 2)
            with sp.Fori(LOOP[0], LOOP[1] - MB + 1, MB) as t0:
                for i in range(MB):
                    load_adj(t0 + i + MB + 2, i % 2)
                    if i % OG == 0:
                        store_ax(t0 + i - OG, OG)
                        store_pair(t0 + i - OG, (i // OG) % 2)
            sp.wait_ge(S["mask_done"], T)
            sp.dma_start(count_dram.rearrange("(p t) o -> p (t o)", p=P), count[:, :]).then_inc(S["count_out"], 16)
            for t in range(LOOP[1] - OG, T - OG, OG):
                store_ax(t, OG)
                store_pair(t, (t // OG) % 2)
            store_ax(T - 2, 1)
            store_ax(T - 1, 1)
            store_pair(T - OG, (T // OG - 1) % 2)
            sp.wait_ge(S["f_row_out"], 16)
            nch = sp.value_load(nch_i[0:1, 0:1], min_val=1, max_val=CH)
            with sp.If(nch > 1):
                with sp.Fori(0, T // OG) as k:
                    sp.wait_ge(S["g_act_norm_done"], k + 2)
                    sp.wait_ge(S["g_dve_norm_done"], k + 2)
                    sp.dma_start(out_tiles[:, bass.ds(k * OG, OG), :],
                                 ax[:, bass.ds(k * OG, OG), :]).then_inc(S["g_out_done"], 16)
                sp.wait_ge(S["g_out_done"], 16 * (T // OG))

        @block.gpsimd
        def _(pool):
            def rows(out_, table, index, done):
                pool.indirect_dma_start(
                    out=out_, out_offset=None, in_=table,
                    in_offset=bass.IndirectOffsetOnAxis(ap=index, axis=0)).then_inc(S[done], 16)

            nc.gpsimd.memset(ones[:, :], 1.0).then_inc(S["const_pool"], 1)
            nc.gpsimd.iota(iota_f[:, :], [[1, P]], base=0, channel_multiplier=0,
                           allow_small_or_imprecise_dtypes=True).then_inc(S["const_pool"], 1)
            nc.gpsimd.iota(slot0[:, :], [[0, 1]], base=0, channel_multiplier=1,
                           allow_small_or_imprecise_dtypes=True).then_inc(S["const_pool"], 1)
            nc.gpsimd.iota(chunk_lo[:, :], [[P, CH]], base=0, channel_multiplier=0,
                           allow_small_or_imprecise_dtypes=True).then_inc(S["const_pool"], 1)
            pool.wait_ge(S["const_pool"], 4)
            nc.gpsimd.affine_select(out=ident[:, :], in_=ones[:, :], compare_op=ALU.is_equal, fill=0.0, base=0,
                                    pattern=[[-1, P]], channel_multiplier=1).then_inc(S["const_pool"], 1)
            nc.gpsimd.affine_select(out=offdiag[:, :], in_=ones[:, :], compare_op=ALU.not_equal, fill=0.0, base=0,
                                    pattern=[[-1, P]], channel_multiplier=1).then_inc(S["const_pool"], 1)
            nc.gpsimd.affine_select(out=before[:, :], in_=ones[:, :], compare_op=ALU.is_gt, fill=0.0, base=0,
                                    pattern=[[-1, P]], channel_multiplier=1).then_inc(S["const_pool"], 1)
            nc.gpsimd.affine_select(out=after[:, :], in_=ones[:, :], compare_op=ALU.is_gt, fill=0.0, base=0,
                                    pattern=[[1, P]], channel_multiplier=-1).then_inc(S["const_pool"], 1)
            pool.wait_ge(S["keys_done"], 1)
            for j in range(EC):
                rows(adjv[0:EP, j:j + 1], adj_flat[:, :], key_i[0:EP, j:j + 1], "adjv_in")
            pool.wait_ge(S["f_idx_done"], 1)
            rows(g[:, 0, :], x[:, :], si[:, 0:1], "f_sub_rows_in")
            rows(g[:, 1, :], x[:, :], si[:, 1:2], "f_obj_rows_in")
            pool.wait_ge(S["f_place_done"], 1)
            pool.wait_ge(S["count_out"], 16)
            rows(count_g[:, :], count_dram, place_i[:, :], "f_count_in")
            pool.wait_ge(S["f_pre_done"], 1)
            pool.wait_ge(S["ax_out"], 16 * (T // OG + 1))
            rows(axg, ax_dram[:, :], si[:, 0:1], "f_ax_in")
            pool.wait_ge(S["f_row_done"], 1)
            pool.wait_ge(S["out_done"], 16 * (T // OG))
            pool.indirect_dma_start(
                out=out[:, :], out_offset=bass.IndirectOffsetOnAxis(ap=row_i[:, :], axis=0), in_=g[:, 0, :],
                in_offset=None, bounds_check=N - 1, oob_is_err=False).then_inc(S["f_row_out"], 16)
            pool.wait_ge(S["nch_done"], 1)
            nch = pool.value_load(nch_i[0:1, 0:1], min_val=1, max_val=CH)
            with pool.If(nch > 1):
                last_pair = pool.to_reg(N * N - 1)
                with pool.Fori(1, nch + 1) as turn:
                    pool.wait_ge(S["nch_done"], 1)
                    pool.wait_ge(S["idx_done"], turn)
                    rows(g[:, 0, :], x[:, :], si[:, 0:1], "sub_rows_in")
                    rows(g[:, 1, :], x[:, :], si[:, 1:2], "obj_rows_in")
                    pool.wait_ge(S["nch_done"], 1)
                    pool.wait_ge(S["skey_done"], turn)
                    pool.indirect_dma_start(
                        out=owner, out_offset=bass.IndirectOffsetOnAxis(ap=skey_i[:, :], axis=0), in_=slot_i[:, :],
                        in_offset=None, bounds_check=last_pair, oob_is_err=False).then_inc(S["owner_out"], 16)
                    pool.wait_ge(S["owner_out"], 16 * turn)
                with pool.Fori(1, nch + 1) as turn:
                    pool.wait_ge(S["nch_done"], 1)
                    pool.wait_ge(S["key2_done"], turn)
                    pool.indirect_dma_start(
                        out=own_g[:, :], out_offset=None, in_=owner,
                        in_offset=bass.IndirectOffsetOnAxis(ap=skey_i[:, :], axis=0),
                        bounds_check=last_pair, oob_is_err=False).then_inc(S["owner_in"], 16)
                with pool.Fori(1, nch + 1) as turn:
                    pool.wait_ge(S["nch_done"], 1)
                    pool.wait_ge(S["obj2_done"], turn)
                    rows(g[:, 1, :], x[:, :], obj_i[:, :], "obj2_rows_in")

        @block.scalar
        def _(act_e):
            a = nc.scalar
            act_e.wait_ge(S["const_dve"], 2)
            a.activation(plain_e0[:, :], self_col[:, :], ACT.Exp, scale=-1.0).then_inc(S["plain_done"], 1)
            a.activation(std[:, 0:1], self_col[:, :], ACT.Copy).then_inc(S["norm_done"], 1)
            a.activation(std[:, 1:2], self_col[:, :], ACT.Copy).then_inc(S["g_act_norm_done"], 1)

            def low_x(i):
                act_e.wait_ge(S["diff_done"], i + 1)
                a.activation(flat(xl[:, i * XG:(i + 1) * XG, :]), diff[:, 0, :], ACT.Copy, scale=LO)\
                    .then_inc(S["xl_done"], 1)

            def copy_quarter(t, b, q):
                act_e.wait_ge(S["tr_done"], Q * t + q + 1)
                a.activation(maskT[:, b, q * TQ:(q + 1) * TQ, :], tp[q % 2][:, :, :], ACT.Copy)\
                    .then_inc(S["copy_done"], 1)

            for i in range(XP):
                act_e.wait_ge(S[f"x_in{i}"], 16)
                a.activation(xh[:, i * XG:(i + 1) * XG, :], xs[:, i * XG:(i + 1) * XG, :], ACT.Copy)\
                    .then_inc(S["xh_done"], 1)
                if i % 2 == 1:
                    low_x(i - 1)
                if i == 3:
                    for q in range(2):
                        copy_quarter(0, 0, q)
                if i == 5:
                    for q in range(2, Q):
                        copy_quarter(0, 0, q)

            def low_out(t, b):
                act_e.wait_ge(S["mm_done"], t + 1)
                act_e.wait_ge(S["ax_done"], t + 1)
                a.activation(low_part[:, b, :], lo_ps[b][:, :], ACT.Copy, scale=1.0 / LO).then_inc(S["low_done"], 1)

            def scaled_x(t, pb_):
                number = t // OG
                act_e.wait_ge(S["cd_done"], number + 1)
                act_e.wait_ge(S["yb_free"], number + 1)
                for i in range(OG):
                    a.activation(yb[:, pb_, i, :], tile_of(xs, t + i), ACT.Copy, scale=dc[:, i:i + 1])\
                        .then_inc(S["t1_done"], 1)

            def std_of(t):
                act_e.wait_ge(S["var_done"], t // OG + 1)
                a.activation(std[:, :], mv[:, :, 1], ACT.Sqrt).then_inc(S["std_done"], 1)

            def normalise(t, pb_):
                act_e.wait_ge(S["norm_ready"], t // OG + 1)
                for i in range(OG):
                    last = a.activation(yb[:, pb_, i, :], yb[:, pb_, i, :], ACT.Identity, scale=rstd[:, i:i + 1],
                                        bias=shift[:, i:i + 1])
                last.then_inc(S["norm_done"], 1)

            def step(t, i, hooks={}):
                ends = i % OG == 0 and not (isinstance(t, int) and t < OG)
                pb_ = ((i - OG) // OG) % 2
                for q in range(Q):
                    if ends and q == 1:
                        scaled_x(t - OG, pb_)
                    if ends and q == 2:
                        std_of(t - OG)
                    if ends and q == 3:
                        normalise(t - OG, pb_)
                    for hook in hooks.get(q, ()):
                        hook()
                    if not (isinstance(t, int) and t == T - 1):
                        copy_quarter(t + 1, (i + 1) % 2, q)
                low_out(t, i % 2)

            def copy_weights():
                for n in range(2 * HT):
                    act_e.wait_ge(S["w_tr"], n + 1)
                    a.activation(wT[:, n // HT, n % HT, :], (ea, eb)[n % 2][:, :], ACT.Copy)\
                        .then_inc(S["w_copied"], 1)

            def copy_gathered(w, turn, k=""):
                tr, cp = (("subT_done", "subT_copied"), ("objT_done", "objT_copied"))[w]
                act_e.wait_ge(S[k + tr], turn)
                a.activation(gT[:, w, :, :].rearrange("p k e -> p (k e)"), (ea, eb)[w][:, :], ACT.Copy)\
                    .then_inc(S[k + cp], 1)

            def edge_exps():
                act_e.wait_ge(S["f_seg_done"], 1)
                a.activation(pexp[:, :], dlt[:, :], ACT.Exp).then_inc(S["f_exp_done"], 1)
                a.activation(x0[:, :], seg[:, :], ACT.Exp, scale=-1.0).then_inc(S["f_exp_done"], 1)
                a.activation(x1[:, :], seg[:, :], ACT.Exp, scale=-1.0, bias=self_col[:, 0:1])\
                    .then_inc(S["f_exp_done"], 1)

            step(0, 0)
            step(1, 1, {0: [copy_weights]})
            with act_e.Fori(LOOP[0], LOOP[1] - MB + 1, MB) as t0:
                for i in range(MB):
                    step(t0 + i, (LOOP[0] + i) % MB)
            ACT_HOOKS = {
                13: {1: [lambda: copy_gathered(0, 1, "f_")], 2: [lambda: copy_gathered(1, 1, "f_")]},
                15: {0: [edge_exps]},
            }
            for t in range(LOOP[1], T):
                step(t, t % MB, ACT_HOOKS.get(t, {}))
            last_pb = (T // OG - 1) % 2
            scaled_x(T - OG, last_pb)
            std_of(T - OG)
            normalise(T - OG, last_pb)
            act_e.wait_ge(S["f_var_done"], 1)
            a.activation(rstd1, var1, ACT.Sqrt).then_inc(S["f_std_done"], 1)

            act_e.wait_ge(S["nch_done"], 1)
            nch = act_e.value_load(nch_i[0:1, 0:1], min_val=1, max_val=CH)
            with act_e.If(nch > 1):
                with act_e.Fori(0, nch) as c:
                    for w in range(2):
                        copy_gathered(w, c + 1)
                with act_e.Fori(0, nch) as c:
                    act_e.wait_ge(S["dlt_done"], c + 1)
                    a.activation(pexp[:, :], dlt[:, :], ACT.Exp).then_inc(S["exp_done"], 1)
                act_e.wait_ge(S["m_final"], 1)
                a.activation(e0[:, :, :], m_st[:, :, :], ACT.Exp, scale=-1.0).then_inc(S["row_exp_done"], 1)
                a.activation(e1[:, :, :], m_st[:, :, :], ACT.Exp, scale=-1.0,
                             bias=self_col[:, 0:1]).then_inc(S["row_exp_done"], 1)
                act_e.wait_ge(S["d1_done"], 1)
                with act_e.Fori(0, T) as t:
                    a.activation(xs[:, bass.ds(t, 1), :], xs[:, bass.ds(t, 1), :], ACT.Copy,
                                 scale=d1[:, bass.ds(t, 1)]).then_inc(S["scaled_done"], 1)
                with act_e.Fori(0, T // OG) as k:
                    act_e.wait_ge(S["g_var_done"], k + 1)
                    a.activation(std[:, :], mv[:, :, 1], ACT.Sqrt).then_inc(S["g_std_done"], 1)
                    act_e.wait_ge(S["g_norm_ready"], k + 1)
                    a.activation(tile_of(ax, k * OG), yb[:, 0, 0, :], ACT.Identity, scale=rstd[:, 0:1],
                                 bias=shift[:, 0:1]).then_inc(S["g_act_norm_done"], 1)

        @block.tensor
        def _(pe):
            pe.wait_ge(S["const_dve"], 1)
            mm = nc.tensor.matmul

            def transposes(t, b, q):
                if q == 0:
                    pe.wait_ge(S["mask_done"], t + 1)
                if not (isinstance(t, int) and t == 0 and q < 2):
                    pe.wait_ge(S["copy_done"], Q * t + q - 1)
                for j in range(TQ):
                    k = q * TQ + j
                    last = mm(tp[q % 2][:, j, :], mask[:, b, k * P:(k + 1) * P], ident16[:, :], start=True, stop=True)
                last.then_inc(S["tr_done"], 1)

            def products(t, b, q):
                pe.wait_ge(S["copy_done"], Q * t + q + 1)
                if q == 0:
                    pe.wait_ge(S["ax_done"], t + 1)
                for j in range(q * TQ, (q + 1) * TQ):
                    if isinstance(t, int) and t == 0 and j % XG == 0:
                        pe.wait_ge(S["xl_done"], j // XG + 1)
                    mm(hi_ps[b][:, :], maskT[:, b, j, :], xh[:, j, :], start=(j == 0), stop=(j == T - 1))
                    last = mm(lo_ps[b][:, :], maskT[:, b, j, :], xl[:, j, :], start=(j == 0), stop=(j == T - 1))
                if q == Q - 1:
                    last.then_inc(S["mm_done"], 1)

            def step(t, i, hooks={}):
                for q in range(Q):
                    for hook in hooks.get(q, ()):
                        hook()
                    if not (isinstance(t, int) and t == T - 1):
                        transposes(t + 1, (i + 1) % MB, q)
                    products(t, i % 2, q)

            def transpose_weights():
                pe.wait_ge(S["w_in"], 32)
                for n in range(2 * HT):
                    if n >= 2:
                        pe.wait_ge(S["w_copied"], n - 1)
                    for o in range(HT):
                        last = nc.tensor.transpose((ea, eb)[n % 2][:, o * P:(o + 1) * P],
                                                   wraw[:, n // HT, o, (n % HT) * P:(n % HT + 1) * P], ident[:, :])
                    last.then_inc(S["w_tr"], 1)

            def slot_offsets():
                pe.wait_ge(S["act_sum_done"], 1)
                mm(eb[:, 0:1], after[0:EP, :], incl[0:EP, EC - 1:EC], start=True, stop=True)
                mm(eb[:, 1:2], ones[0:EP, :], incl[0:EP, EC - 1:EC], start=True, stop=True)\
                    .then_inc(S["offs_done"], 1)

            def compact(part, turn, k=""):
                pe.wait_ge(S[k + "onehot_done"], turn)
                for j in range(CG):
                    n = part * CG + j
                    last = mm(ea[:, 0:3], onehot[0:EP, part % 2, j, :], so16[0:EP, n, :],
                              start=(n == 0), stop=(n == EC - 1))
                last.then_inc(S[k + "compact_part"], 1)

            def keys_across(turn, k=""):
                pe.wait_ge(S[k + "kb_done"], turn)
                for w in range(2):
                    last = nc.tensor.transpose(eb[:, w * P:(w + 1) * P], kb[:, w, :], ident[:, :])
                last.then_inc(S[k + "keyT_done"], 1)

            def gathered_across(w, turn, k=""):
                pe.wait_ge(S[k + ("sub_rows_in", "obj_rows_in")[w]], 16 * turn)
                if w == 1:
                    pe.wait_ge(S[k + "keyT_used"], turn)
                for i in range(HT):
                    last = nc.tensor.transpose((ea, eb)[w][:, i * P:(i + 1) * P], g[:, w, i * P:(i + 1) * P],
                                               ident[:, :])
                last.then_inc(S[k + ("subT_done", "objT_done")[w]], 1)

            def project(w, turn, k=""):
                pe.wait_ge(S[k + ("subT_copied", "objT_copied")[w]], turn)
                for i in range(HT):
                    last = mm((ea, eb)[w][:, :], gT[:, w, i, :], wT[:, w, i, :], start=(i == 0), stop=(i == HT - 1))
                last.then_inc(S[k + ("q_done", "k_done")[w]], 1)

            def scores_across(turn, k=""):
                pe.wait_ge(S[k + "attB_done"], turn)
                for h in range(HEADS):
                    ps = (ea, eb)[h // 4]
                    last = nc.tensor.transpose(ps[:, (h % 4) * P:(h % 4 + 1) * P], attB[:, h, :], ident[:, :])
                last.then_inc(S[k + "attT_done"], 1)

            def edge_sums():
                pe.wait_ge(S["f_e9_done"], 1)
                mm(ea[:, 0:HEADS + 1], same[:, :], e9[:, :], start=True, stop=True).then_inc(S["f_z_done"], 1)

            def edge_rows():
                pe.wait_ge(S["f_sameW_done"], 1)
                mm(eb[:, :], sameW, g[:, 1, :], start=True, stop=True).then_inc(S["f_edges_done"], 1)

            for q in range(Q):
                transposes(0, 0, q)
            step(0, 0)
            step(1, 1, {0: [transpose_weights]})
            with pe.Fori(LOOP[0], LOOP[1] - MB + 1, MB) as t0:
                for i in range(MB):
                    step(t0 + i, (LOOP[0] + i) % MB)
            f = "f_"
            PE_HOOKS = {
                10: {1: [slot_offsets]},
                11: {0: [lambda: compact(0, 1, f)], 1: [lambda: compact(1, 2, f)], 3: [lambda: compact(2, 3, f)]},
                12: {0: [lambda: compact(3, 4, f)], 1: [lambda: compact(4, 5, f)], 3: [lambda: keys_across(1, f)]},
                13: {1: [lambda: gathered_across(0, 1, f)], 2: [lambda: gathered_across(1, 1, f)],
                     3: [lambda: project(0, 1, f)]},
                14: {0: [lambda: project(1, 1, f)], 2: [lambda: scores_across(1, f)]},
                15: {1: [edge_sums], 3: [edge_rows]},
            }
            for t in range(LOOP[1], T):
                step(t, t % MB, PE_HOOKS.get(t, {}))

            pe.wait_ge(S["nch_done"], 1)
            nch = pe.value_load(nch_i[0:1, 0:1], min_val=1, max_val=CH)
            with pe.If(nch > 1):
                with pe.Fori(0, nch) as c:
                    for part in range(NG):
                        compact(part, c * NG + part + 1)
                    keys_across(c + 1)
                    for w in range(2):
                        gathered_across(w, c + 1)
                    for w in range(2):
                        project(w, c + 1)
                    scores_across(c + 1)
                    pe.wait_ge(S["maxspread_done"], c + 1)
                    mm(ea[:, 0:T * HEADS], hot_lo[:, :], flat(spread8[:, :, :]),
                       start=True, stop=True).then_inc(S["max_done"], 1)
                with pe.Fori(0, nch) as c:
                    pe.wait_ge(S["hotlo_done"], c + 1)
                    nc.tensor.transpose(eb[:, 0:P], hot_lo[:, :], ident[:, :]).then_inc(S["hotloT_done"], 1)
                    pe.wait_ge(S["hotloT_copied"], c + 1)
                    mm(ea[:, 0:T * HEADS], hot_loT[:, :], flat(m_st[:, :, :]),
                       start=True, stop=True).then_inc(S["mG_done"], 1)
                    pe.wait_ge(S["zspread_done"], c + 1)
                    mm(eb[:, 0:T * (HEADS + 1)], hot_lo[:, :], flat(spread[:, :, :]),
                       start=True, stop=True).then_inc(S["z_done"], 1)
                with pe.Fori(0, nch) as c:
                    pe.wait_ge(S["hotlo3_done"], c + 1)
                    nc.tensor.transpose(eb[:, 0:P], hot_lo[:, :], ident[:, :]).then_inc(S["hotloT3_done"], 1)
                    pe.wait_ge(S["hotloT3_copied"], c + 1)
                    mm(ea[:, 0:T * (HEADS + 1)], hot_loT[:, :], flat(rz_st[:, :, :]),
                       start=True, stop=True).then_inc(S["rzG_done"], 1)
                    pe.wait_ge(S["wL_done"], c + 1)
                    pe.wait_ge(S["obj2_rows_in"], 16 * (c + 1))
                    for t in range(T):
                        if t >= 2:
                            pe.wait_ge(S["edge_added"], c * T + t - 1)
                        mm((ea, eb)[t % 2][:, :], wL[:, t, :], g[:, 1, :], start=True, stop=True)\
                            .then_inc(S["edge_mm_done"], 1)

        @block.vector
        def _(dve):
            v = nc.vector
            setup = Chain(dve, S["dve_setup"])
            v.memset(self_col[:, :], SELF).then_inc(S["const_dve"], 1)
            v.memset(zeros[:, :], 0.0).then_inc(S["ax_done"], 2)
            v.memset(own_g[:, :], -1).then_inc(S["yb_free"], 2)
            v.memset(m_st[:, :, :], SELF).then_inc(S["g_dve_norm_done"], 1)
            v.memset(z_st[:, :, :], 0.0)
            setup(v.memset(so16[:, :, :], 1.0))
            dve.wait_ge(S["pairs_in"], 16)
            setup(v.tensor_copy(prf[0:EP], pr[0:EP]))
            setup(v.scalar_tensor_tensor(out=keyf[0:EP], in0=prf[0:EP, :, 0], scalar=float(N), in1=prf[0:EP, :, 1],
                                         op0=ALU.mult, op1=ALU.add))
            v.tensor_copy(key_i[0:EP], keyf[0:EP]).then_inc(S["keys_done"], 1)
            v.tensor_copy(so16[0:EP, :, 0:2], prf[0:EP])
            dve.wait_ge(S["const_pool"], 8)
            v.tensor_copy(iota16[:, :], iota_f[:, :])
            v.tensor_copy(ident16[:, :], ident[:, :]).then_inc(S["const_dve"], 1)

            def make_mask(t, i, link):
                b = i % 2
                dve.wait_ge(S[f"adj_in{b}"], 8 * (t - b) + 16)
                diag = adjf[:, b, t * P:(t + 1) * P] if isinstance(t, int) else adjf[:, b, bass.ds(t * P, P)]
                link(v.tensor_tensor(diag, diag, offdiag[:, :], ALU.mult))
                if not isinstance(t, int) or t >= MB:
                    dve.wait_ge(S["tr_done"], Q * (t - MB + 1))
                n = count[:, t:t + 1] if isinstance(t, int) else count[:, bass.ds(t, 1)]
                v.tensor_scalar(mask[:, i % MB, :], adjf[:, b, :], 1.0, 0.0, ALU.is_equal, ALU.add, accum_out=n)\
                    .then_inc(S["mask_done"], 1)

            def sum_halves(t, b):
                dve.wait_ge(S["low_done"], t + 1)
                v.tensor_tensor(tile_of(ax, t), hi_ps[b][:, :], low_part[:, b, :], ALU.add)\
                    .then_inc(S["ax_done"], 1)

            PLAIN = 7

            def plain_weights(t, link):
                dve.wait_ge(S["mask_done"], t + OG)
                n = count[:, t:t + OG] if isinstance(t, int) else count[:, bass.ds(t, OG)]
                link(v.tensor_scalar(zc[:, :], n, plain_e0[:, 0:1], 1.0, ALU.mult, ALU.add))
                link(v.reciprocal(zc[:, :], zc[:, :]))
                v.tensor_scalar(cc[:, :], zc[:, :], plain_e0[:, 0:1], None, ALU.mult)
                v.tensor_scalar(dc[:, :], zc[:, :], 1.0, None, ALU.add).then_inc(S["cd_done"], 1)

            def plain_rows(t, pb_, link):
                dve.wait_ge(S["ax_done"], t + OG + 2)
                for i in range(OG):
                    dve.wait_ge(S["t1_done"], t + i + 1)
                    ins = v.scalar_tensor_tensor(out=yb[:, pb_, i, :], in0=tile_of(ax, t + i), scalar=cc[:, i:i + 1],
                                                 in1=yb[:, pb_, i, :], op0=ALU.mult, op1=ALU.add)
                link(ins)
                for i in range(OG):
                    ins = v.bn_stats(stats[:, i, :], yb[:, pb_, i, :])
                link(ins)
                v.memset(junk[:, 0:1], 0.0)
                for i in range(OG):
                    ins = v.bn_aggr(mv[:, i, :], stats[:, i, :])
                link(ins)
                v.tensor_scalar(mv[:, :, 1], mv[:, :, 1], EPS, None, ALU.add).then_inc(S["var_done"], 1)

            def plain_scale(t, link):
                dve.wait_ge(S["std_done"], t // OG + 1)
                dve.wait_ge(S["norm_done"], t // OG + 1)
                link(v.reciprocal(rstd[:, :], std[:, :]))
                link(v.tensor_tensor(shift[:, :], mv[:, :, 0], rstd[:, :], ALU.mult))
                v.tensor_scalar(shift[:, :], shift[:, :], -1.0, None, ALU.mult).then_inc(S["norm_ready"], 1)

            def chain_of_pair(t):
                return Chain(dve, S["dve_plain"], t // OG * PLAIN)

            def step(t, i, hooks={}):
                for hook in hooks.get("first", ()):
                    hook()
                ends = i % OG == 0 and not (isinstance(t, int) and t < OG)
                pb_ = ((i - OG) // OG) % 2
                if ends:
                    pair = Chain(dve, S["dve_plain"], (t - OG) // OG * PLAIN + 2)
                    plain_rows(t - OG, pb_, pair)
                for hook in hooks.get("rows", ()):
                    hook()
                if not (isinstance(t, int) and t + MB >= T):
                    make_mask(t + MB, i, Chain(dve, S["dve_tile"], t + MB))
                if ends:
                    plain_scale(t - OG, pair)
                    assert pair.n == PLAIN - 2
                if i % OG == OG - 1:
                    plain_weights(t - OG + 1, Chain(dve, S["dve_plain"], (t - OG + 1) // OG * PLAIN))
                for hook in hooks.get("sum", ()):
                    hook()
                sum_halves(t, i % 2)

            valid = se[:, 2:3]

            def one_hot(part, number, k=""):
                if not isinstance(number, int) or number > 2:
                    dve.wait_ge(S[k + "compact_part"], number - 2)
                cols_ = slice(part * CG, (part + 1) * CG)
                v.tensor_tensor(onehot[0:EP, part % 2], times(iota16[0:EP, :], CG), wide(slot16[0:EP, cols_], P),
                                ALU.is_equal).then_inc(S[k + "onehot_done"], 1)

            def locate(step_, turn, k=""):
                dve.wait_ge(S[k + "compact_part"], NG * turn)
                step_(v.tensor_copy(se[:, :], ea[:, 0:3]))
                step_(v.tensor_copy(si[:, :], se[:, 0:2]))
                v.scalar_tensor_tensor(out=keyv, in0=se[:, 0:1], scalar=float(N), in1=se[:, 1:2],
                                       op0=ALU.mult, op1=ALU.add).then_inc(S[k + "idx_done"], 1)
                v.tensor_scalar(split_i[:, 0:1], si[:, 0:1], 7, None, ALU.arith_shift_right)
                step_(v.tensor_scalar(split_i[:, 1:2], si[:, 0:1], P - 1, None, ALU.bitwise_and))
                step_(v.tensor_copy(split_f[:, :], split_i[:, :]))
                v.tensor_scalar(keyv, keyv, 1.0, valid, ALU.add, ALU.mult)
                v.tensor_scalar(subv, se[:, 0:1], 1.0, valid, ALU.add, ALU.mult)
                step_(v.tensor_scalar(hiv, split_f[:, 0:1], 1.0, valid, ALU.add, ALU.mult))
                step_(v.tensor_scalar(cols[:, 0:2], cols[:, 0:2], -1.0, None, ALU.add))
                step_(v.tensor_scalar(hiv, hiv, -1.0, None, ALU.add))
                v.tensor_copy(kb[:, :, :], wide(cols[:, 0:2], P)).then_inc(S[k + "kb_done"], 1)

            def repeats(step_, turn, k=""):
                dve.wait_ge(S[k + "keyT_done"], turn)
                step_(v.scalar_tensor_tensor(out=junk[:, :], in0=eb[:, 0:P], scalar=keyv, in1=before[:, :],
                                             op0=ALU.is_equal, op1=ALU.mult, accum_out=dup))
                v.tensor_scalar(same[:, :], eb[:, P:2 * P], subv, None, ALU.is_equal).then_inc(S[k + "keyT_used"], 1)
                dve.wait_ge(S[k + "keyT_used"], turn)
                step_(v.scalar_tensor_tensor(out=junk[:, :], in0=same[:, :], scalar=1.0, in1=before[:, :],
                                             op0=ALU.mult, op1=ALU.mult, accum_out=cnt))
                v.tensor_scalar(uniq, dup, 0.0, valid, ALU.is_equal, ALU.mult)
                step_(v.tensor_scalar(rep, cnt, 0.0, valid, ALU.is_equal, ALU.mult))

            def score(step_, turn, k=""):
                for w, done in enumerate(("q_done", "k_done")):
                    dve.wait_ge(S[k + done], turn)
                    ins = v.tensor_tensor(qk[:, w, :], (ea, eb)[w][:, :], bias[:, w, :], ALU.add)
                step_(ins)
                step_(v.tensor_tensor(qk[:, 2, :], qk[:, 0, :], qk[:, 1, :], ALU.mult))
                step_(v.tensor_reduce(att1[:, :], qk[:, 2, :].rearrange("p (h d) -> p h d", h=HEADS), AX.X, ALU.add))
                step_(v.tensor_scalar(att1[:, :], att1[:, :], DK ** -0.5, valid, ALU.mult, ALU.mult))
                v.tensor_copy(attB[:, :, :], wide(att1[:, :], P)).then_inc(S[k + "attB_done"], 1)

            def largest(step_, turn, k=""):
                dve.wait_ge(S[k + "attT_done"], turn)
                for i, ps in enumerate((ea, eb)):
                    ins = v.tensor_tensor(attM[:, 4 * i:4 * i + 4, :], ps[:, :].rearrange("p (h e) -> p h e", h=4),
                                          times(same[:, :], 4), ALU.mult)
                step_(ins)
                step_(v.tensor_reduce(seg[:, :], attM[:, :, :], AX.X, ALU.max))

            fast = Chain(dve, S["dve_fast"])
            f = "f_"

            def find_active():
                fast(v.tensor_tensor(act[0:EP], prf[0:EP, :, 0], prf[0:EP, :, 1], ALU.not_equal))
                dve.wait_ge(S["adjv_in"], 16 * EC)
                fast(v.scalar_tensor_tensor(out=act[0:EP], in0=adjv[0:EP], scalar=1.0, in1=act[0:EP],
                                            op0=ALU.is_equal, op1=ALU.mult))
                v.tensor_tensor_scan(out=incl[0:EP], data0=act[0:EP], data1=zeros[0:EP], initial=0.0,
                                     op0=ALU.add, op1=ALU.add).then_inc(S["act_sum_done"], 1)

            def make_slots():
                dve.wait_ge(S["offs_done"], 1)
                fast(v.tensor_copy(offs[:, :], eb[:, 0:2]))
                fast(v.tensor_scalar(chunk_tmp[:, :], chunk_lo[:, :], offs[:, 1:2], 0.0, ALU.is_lt, ALU.add,
                                     accum_out=nch_f[:, 0:1]))
                v.tensor_scalar(nch_f[:, 1:2], nch_f[:, 0:1], 1.0, None, ALU.max)
                fast(v.tensor_scalar(slot[0:EP], incl[0:EP], offs[0:EP, 0:1], None, ALU.add))
                v.tensor_copy(nch_i[:, :], nch_f[:, 1:2]).then_inc(S["nch_done"], 1)
                fast(v.tensor_tensor(slot[0:EP], slot[0:EP], act[0:EP], ALU.mult))
                fast(v.tensor_scalar(slot[0:EP], slot[0:EP], -1.0, None, ALU.add))
                fast(v.tensor_scalar(slot16[0:EP], slot[0:EP], -1.0, float(P), ALU.max, ALU.min))
                one_hot(0, 1, f)
                one_hot(1, 2, f)

            def place_rows():
                locate(fast, 1, f)
                fast(v.scalar_tensor_tensor(out=place_f, in0=split_f[:, 1:2], scalar=float(T), in1=split_f[:, 0:1],
                                            op0=ALU.mult, op1=ALU.add))
                v.tensor_copy(place_i[:, :], place_f).then_inc(S["f_place_done"], 1)

            def find_repeats():
                repeats(fast, 1, f)
                fast(v.tensor_scalar(row_f, rep, -PAST, PAST, ALU.mult, ALU.add))
                fast(v.tensor_tensor(row_f, row_f, se[:, 0:1], ALU.add))
                fast(v.tensor_copy(row_i[:, :], row_f))

            def row_maximum():
                largest(fast, 1, f)
                fast(v.tensor_scalar(seg[:, :], seg[:, :], SELF, None, ALU.max))
                v.tensor_tensor(dlt[:, :], att1[:, :], seg[:, :], ALU.subtract).then_inc(S["f_seg_done"], 1)
                v.tensor_copy(e9[:, HEADS:HEADS + 1], uniq)
                dve.wait_ge(S["f_exp_done"], 3)
                v.tensor_scalar(e9[:, 0:HEADS], pexp[:, :], uniq, None, ALU.mult).then_inc(S["f_e9_done"], 1)

            def row_weights():
                dve.wait_ge(S["f_z_done"], 1)
                dve.wait_ge(S["f_e9_done"], 1)
                dve.wait_ge(S["f_count_in"], 16)
                fast(v.tensor_tensor(n_edge, count_g[:, :], ea[:, HEADS:HEADS + 1], ALU.subtract))
                fast(v.scalar_tensor_tensor(out=xz[:, :], in0=x0[:, :], scalar=n_edge, in1=x1[:, :],
                                            op0=ALU.mult, op1=ALU.add))
                fast(v.tensor_tensor(xz[:, :], xz[:, :], ea[:, 0:HEADS], ALU.add))
                fast(v.reciprocal(xz[:, :], xz[:, :]))
                fast(v.tensor_scalar(xz[:, :], xz[:, :], 1.0 / HEADS, None, ALU.mult))
                v.scalar_tensor_tensor(out=x0[:, :], in0=x0[:, :], scalar=1.0, in1=xz[:, :], op0=ALU.mult,
                                       op1=ALU.mult, accum_out=c_edge)
                v.scalar_tensor_tensor(out=x1[:, :], in0=x1[:, :], scalar=1.0, in1=xz[:, :], op0=ALU.mult,
                                       op1=ALU.mult, accum_out=d_edge)
                fast(v.scalar_tensor_tensor(out=dlt[:, :], in0=e9[:, 0:HEADS], scalar=1.0, in1=xz[:, :],
                                            op0=ALU.mult, op1=ALU.mult, accum_out=wcol))
                v.tensor_scalar(d_edge, d_edge, 1.0, None, ALU.add)
                fast(v.tensor_scalar(wcol, wcol, c_edge, uniq, ALU.subtract, ALU.mult))
                v.tensor_scalar(sameW, same[:, :], wcol, None, ALU.mult).then_inc(S["f_sameW_done"], 1)

            def rows_but_ax():
                dve.wait_ge(S["f_edges_done"], 1)
                v.scalar_tensor_tensor(out=g[:, 0, :], in0=g[:, 0, :], scalar=d_edge, in1=eb[:, :],
                                       op0=ALU.mult, op1=ALU.add).then_inc(S["f_pre_done"], 1)

            def finish_rows():
                dve.wait_ge(S["f_pre_done"], 1)
                dve.wait_ge(S["f_ax_in"], 16)
                fast(v.scalar_tensor_tensor(out=g[:, 0, :], in0=axg, scalar=c_edge, in1=g[:, 0, :],
                                            op0=ALU.mult, op1=ALU.add))
                fast(v.bn_stats(st1[:, :], g[:, 0, :]))
                fast(v.bn_aggr(mv1[:, :], st1[:, :]))
                v.tensor_scalar(var1, mv1[:, 1:2], EPS, None, ALU.add).then_inc(S["f_var_done"], 1)
                dve.wait_ge(S["f_std_done"], 1)
                fast(v.reciprocal(rstd1, rstd1))
                v.tensor_scalar(g[:, 0, :], g[:, 0, :], mv1[:, 0:1], rstd1, ALU.subtract, ALU.mult)\
                    .then_inc(S["f_row_done"], 1)

            tile = Chain(dve, S["dve_tile"])
            for i in range(XP):
                piece = slice(i * XG, (i + 1) * XG)
                dve.wait_ge(S["xh_done"], i + 1)
                if i >= 2:
                    dve.wait_ge(S["xl_done"], i - 1)
                ins = v.tensor_tensor(diff[:, i % 2, :], flat(xs[:, piece, :]), flat(xh[:, piece, :]), ALU.subtract)
                ins.then_inc(S["diff_done"], 1)
                if i % 2 == 1:
                    dve.wait_ge(S["diff_done"], i + 1)
                    dve.wait_ge(S["xl_done"], i)
                    v.tensor_scalar(flat(xl[:, piece, :]), diff[:, 1, :], LO, None, ALU.mult)\
                        .then_inc(S["xl_done"], 1)
                if i == 2:
                    make_mask(0, 0, tile)
                if i == 5:
                    make_mask(1, 1, tile)
            make_mask(2, 2, tile)
            make_mask(3, 3, tile)
            dve.wait_ge(S["plain_done"], 1)
            dve.wait_ge(S["w_copied"], 2 * HT)
            step(0, 0)
            step(1, 1)
            with dve.Fori(LOOP[0], LOOP[1] - MB + 1, MB) as t0:
                for i in range(MB):
                    step(t0 + i, (LOOP[0] + i) % MB)
            DVE_HOOKS = {
                10: {"first": [find_active], "rows": [make_slots]},
                11: {"sum": [lambda: one_hot(2, 3, f), lambda: one_hot(3, 4, f)]},
                12: {"rows": [lambda: one_hot(4, 5, f), place_rows]},
                13: {"sum": [find_repeats]},
                14: {"sum": [lambda: score(fast, 1, f)]},
                15: {"first": [row_maximum], "sum": [row_weights]},
            }
            for t in range(LOOP[1], T):
                if t == 11:
                    dve.wait_ge(S["bias_in"], 32)
                step(t, t % MB, DVE_HOOKS.get(t, {}))
            rows_but_ax()
            last_pb = (T // OG - 1) % 2
            pair = Chain(dve, S["dve_plain"], (T - OG) // OG * PLAIN + 2)
            plain_rows(T - OG, last_pb, pair)
            plain_scale(T - OG, pair)
            finish_rows()

            dve.wait_ge(S["f_row_out"], 16)
            nch = dve.value_load(nch_i[0:1, 0:1], min_val=1, max_val=CH)

            def column(c, i):
                return flat(col_all[:, bass.ds(c, 1), i:i + 1])

            def heads_of(tensor, c):
                return flat(tensor[:, bass.ds(c, 1), :])

            with dve.If(nch > 1):
                start = Chain(dve, S["dve_flags"])
                start(v.tensor_copy(slotv, slot0[:, :]))
                STEPS1 = 25
                with dve.Fori(0, nch) as c:
                    step1 = Chain(dve, S["dve_scan"], c * STEPS1)
                    step1(v.tensor_scalar(slot16[0:EP], slot[0:EP], -1.0, float(P), ALU.max, ALU.min))
                    for part in range(NG):
                        one_hot(part, part + 1 if part < 2 else c * NG + part + 1)
                    step1(v.tensor_scalar(slot[0:EP], slot[0:EP], -float(P), None, ALU.add))
                    locate(step1, c + 1)
                    v.tensor_copy(column(c, 0), hiv)
                    v.tensor_copy(column(c, 1), split_f[:, 1:2])
                    v.tensor_copy(column(c, 2), se[:, 1:2])
                    v.tensor_copy(column(c, 3), valid)
                    v.tensor_scalar(hot_hi[:, :], iota_f[:, 0:T], hiv, None, ALU.is_equal)
                    step1(v.tensor_scalar(hot_lo[:, :], iota_f[:, :], split_f[:, 1:2], None, ALU.is_equal))
                    repeats(step1, c + 1)
                    step1(v.tensor_scalar(k2, uniq, -PAST, PAST, ALU.mult, ALU.add))
                    step1(v.tensor_tensor(skey_f, keyv, k2, ALU.add))
                    step1(v.tensor_scalar(skey_f, skey_f, -1.0, None, ALU.max))
                    v.tensor_copy(slot_i[:, :], slotv)
                    v.tensor_copy(skey_i[:, :], skey_f).then_inc(S["skey_done"], 1)
                    score(step1, c + 1)
                    v.tensor_copy(heads_of(att_all, c), att1[:, :])
                    largest(step1, c + 1)
                    step1(v.tensor_scalar(seg[:, :], seg[:, :], rep, None, ALU.mult))
                    v.tensor_tensor(spread8[:, :, :], wide(hot_hi[:, :], HEADS), times(seg[:, :], T), ALU.mult)\
                        .then_inc(S["maxspread_done"], 1)
                    dve.wait_ge(S["max_done"], c + 1)
                    step1(v.tensor_tensor(m_st[:, :, :], m_st[:, :, :],
                                          ea[:, 0:T * HEADS].rearrange("p (t h) -> p t h", h=HEADS), ALU.max))
                    dve.wait_ge(S["owner_out"], 16 * (c + 1))
                    step1(v.tensor_scalar(slotv, slotv, float(P), None, ALU.add))
                    assert step1.n == STEPS1, step1.n
                v.tensor_copy(junk[:, 0:1], self_col[:, :]).then_inc(S["m_final"], 1)

                again = Chain(dve, S["dve_exp"])
                again(v.tensor_copy(slotv, slot0[:, :]))
                STEPS2 = 12
                with dve.Fori(0, nch) as c:
                    step2 = Chain(dve, S["dve_exp"], c * STEPS2 + 1)
                    v.tensor_scalar(hot_hi[:, :], iota_f[:, 0:T], column(c, 0), None, ALU.is_equal)
                    v.tensor_scalar(hot_lo[:, :], iota_f[:, :], column(c, 1), None, ALU.is_equal)\
                        .then_inc(S["hotlo_done"], 1)
                    step2(v.scalar_tensor_tensor(out=subv, in0=column(c, 0), scalar=float(P), in1=column(c, 1),
                                                 op0=ALU.mult, op1=ALU.add))
                    step2(v.scalar_tensor_tensor(out=keyv, in0=subv, scalar=float(N), in1=column(c, 2),
                                                 op0=ALU.mult, op1=ALU.add))
                    step2(v.tensor_scalar(k2, column(c, 3), -PAST, PAST, ALU.mult, ALU.add))
                    step2(v.tensor_tensor(skey_f, keyv, k2, ALU.add))
                    v.tensor_copy(skey_i[:, :], skey_f).then_inc(S["key2_done"], 1)
                    dve.wait_ge(S["hotloT_done"], c + 1)
                    v.tensor_copy(hot_loT[:, :], eb[:, 0:P]).then_inc(S["hotloT_copied"], 1)
                    dve.wait_ge(S["mG_done"], c + 1)
                    step2(v.tensor_tensor(spread8[:, :, :], ea[:, 0:T * HEADS].rearrange("p (t h) -> p t h", h=HEADS),
                                          wide(hot_hi[:, :], HEADS), ALU.mult))
                    step2(v.tensor_reduce(seg[:, :], spread8[:, :, :].rearrange("p t h -> p h t"), AX.X, ALU.add))
                    v.tensor_tensor(dlt[:, :], heads_of(att_all, c), seg[:, :], ALU.subtract)\
                        .then_inc(S["dlt_done"], 1)
                    dve.wait_ge(S["owner_in"], 16 * (c + 1))
                    step2(v.tensor_copy(own_f[:, :], own_g[:, :]))
                    step2(v.tensor_tensor(owned, own_f[:, :], slotv, ALU.is_equal))
                    step2(v.tensor_tensor(owned, owned, column(c, 3), ALU.mult))
                    step2(v.tensor_scalar(slotv, slotv, float(P), None, ALU.add))
                    v.tensor_copy(column(c, 5), owned)
                    v.tensor_copy(e9[:, HEADS:HEADS + 1], owned)
                    dve.wait_ge(S["exp_done"], c + 1)
                    step2(v.tensor_scalar(e9[:, 0:HEADS], pexp[:, :], owned, None, ALU.mult))
                    v.tensor_copy(heads_of(p_all, c), e9[:, 0:HEADS])
                    v.tensor_tensor(spread[:, :, :], wide(hot_hi[:, :], HEADS + 1), times(e9[:, :], T), ALU.mult)\
                        .then_inc(S["zspread_done"], 1)
                    dve.wait_ge(S["z_done"], c + 1)
                    step2(v.tensor_tensor(z_st[:, :, :], z_st[:, :, :],
                                          eb[:, 0:T * (HEADS + 1)].rearrange("p (t h) -> p t h", h=HEADS + 1),
                                          ALU.add))
                    assert step2.n == STEPS2, step2.n

                rows = Chain(dve, S["dve_rows"])
                rows(v.tensor_tensor(n0[:, :], count[:, :], z_st[:, :, HEADS], ALU.subtract))
                dve.wait_ge(S["row_exp_done"], 2)
                rows(v.tensor_tensor(rt[:, :, :], e0[:, :, :], wide(n0[:, :], HEADS), ALU.mult))
                rows(v.tensor_tensor(rt[:, :, :], rt[:, :, :], e1[:, :, :], ALU.add))
                rows(v.tensor_tensor(rt[:, :, :], rt[:, :, :], z_st[:, :, 0:HEADS], ALU.add))
                rows(v.reciprocal(rt[:, :, :], rt[:, :, :]))
                rows(v.tensor_scalar(rz_st[:, :, 0:HEADS], rt[:, :, :], 1.0 / HEADS, None, ALU.mult))
                rows(v.tensor_tensor(rt[:, :, :], rz_st[:, :, 0:HEADS], e1[:, :, :], ALU.mult))
                rows(v.tensor_reduce(d1[:, :], rt[:, :, :], AX.X, ALU.add))
                v.tensor_scalar(d1[:, :], d1[:, :], 1.0, None, ALU.add).then_inc(S["d1_done"], 1)
                rows(v.tensor_tensor(e0[:, :, :], rz_st[:, :, 0:HEADS], e0[:, :, :], ALU.mult))
                rows(v.tensor_reduce(rz_st[:, :, HEADS], e0[:, :, :], AX.X, ALU.add))
                dve.wait_ge(S["scaled_done"], T)

                STEPS3 = 6
                with dve.Fori(0, nch) as c:
                    step3 = Chain(dve, S["dve_edges"], c * STEPS3)
                    v.tensor_copy(obj_i[:, :], column(c, 2)).then_inc(S["obj2_done"], 1)
                    v.tensor_scalar(hot_hi[:, :], iota_f[:, 0:T], column(c, 0), None, ALU.is_equal)
                    v.tensor_scalar(hot_lo[:, :], iota_f[:, :], column(c, 1), None, ALU.is_equal)\
                        .then_inc(S["hotlo3_done"], 1)
                    dve.wait_ge(S["hotloT3_done"], c + 1)
                    v.tensor_copy(hot_loT[:, :], eb[:, 0:P]).then_inc(S["hotloT3_copied"], 1)
                    dve.wait_ge(S["rzG_done"], c + 1)
                    step3(v.tensor_tensor(spread[:, :, :],
                                          ea[:, 0:T * (HEADS + 1)].rearrange("p (t h) -> p t h", h=HEADS + 1),
                                          wide(hot_hi[:, :], HEADS + 1), ALU.mult))
                    step3(v.tensor_reduce(e9[:, :], spread[:, :, :].rearrange("p t h -> p h t"), AX.X, ALU.add))
                    step3(v.tensor_tensor(dlt[:, :], heads_of(p_all, c), e9[:, 0:HEADS], ALU.mult))
                    step3(v.tensor_reduce(wcol, dlt[:, :], AX.X, ALU.add))
                    step3(v.tensor_scalar(wcol, wcol, e9[:, HEADS:HEADS + 1], column(c, 5), ALU.subtract, ALU.mult))
                    step3(v.tensor_scalar(hot_hi[:, :], hot_hi[:, :], wcol, None, ALU.mult))
                    v.tensor_tensor(wL[:, :, :], times(hot_lo[:, :], T), wide(hot_hi[:, :], P), ALU.mult)\
                        .then_inc(S["wL_done"], 1)
                    for t in range(T):
                        dve.wait_ge(S["edge_mm_done"], c * T + t + 1)
                        v.tensor_tensor(xs[:, t, :], xs[:, t, :], (ea, eb)[t % 2][:, :], ALU.add)\
                            .then_inc(S["edge_added"], 1)
                    dve.wait_ge(S["edge_added"], c * T + T)
                    assert step3.n == STEPS3, step3.n

                NSTEPS = 5
                with dve.Fori(0, T // OG) as k:
                    step4 = Chain(dve, S["dve_norm"], k * NSTEPS)
                    dve.wait_ge(S["g_act_norm_done"], k + 1)
                    dve.wait_ge(S["g_dve_norm_done"], k + 1)
                    for i in range(OG):
                        t1 = bass.ds(k * OG + i, 1)
                        ins = v.scalar_tensor_tensor(out=yb[:, 0, i, :], in0=tile_of(ax, k * OG + i),
                                                     scalar=flat(rz_st[:, t1, HEADS:HEADS + 1]),
                                                     in1=tile_of(xs, k * OG + i), op0=ALU.mult, op1=ALU.add)
                    step4(ins)
                    for i in range(OG):
                        ins = v.bn_stats(stats[:, i, :], yb[:, 0, i, :])
                    step4(ins)
                    v.memset(junk[:, 0:1], 0.0)
                    for i in range(OG):
                        ins = v.bn_aggr(mv[:, i, :], stats[:, i, :])
                    step4(ins)
                    v.tensor_scalar(mv[:, :, 1], mv[:, :, 1], EPS, None, ALU.add).then_inc(S["g_var_done"], 1)
                    dve.wait_ge(S["g_std_done"], k + 1)
                    step4(v.reciprocal(rstd[:, :], std[:, :]))
                    step4(v.tensor_tensor(shift[:, :], mv[:, :, 0], rstd[:, :], ALU.mult))
                    v.tensor_scalar(shift[:, :], shift[:, :], -1.0, None, ALU.mult).then_inc(S["g_norm_ready"], 1)
                    dve.wait_ge(S["g_norm_ready"], k + 1)
                    v.tensor_scalar(tile_of(ax, k * OG + 1), yb[:, 0, 1, :], rstd[:, 1:2], shift[:, 1:2],
                                    ALU.mult, ALU.add).then_inc(S["g_dve_norm_done"], 1)
                    assert step4.n == NSTEPS, step4.n


_INS = ['x', 'adj', 'L0_gnn_rel_pair_index', 'L0_gnn_Wq', 'L0_gnn_bq', 'L0_gnn_Wk', 'L0_gnn_bk']
_OUTS = [((2048, 512), 'float32')]


def kernel(**inputs):
    import numpy as _np
    import concourse.bacc as _bacc
    from concourse import mybir as _mybir
    from concourse.bass_utils import run_bass_kernel_spmd as _run

    nc = _bacc.Bacc("TRN2", target_bir_lowering=False, num_devices=1)
    arrays, args = {}, []
    for name in _INS:
        a = _np.ascontiguousarray(inputs[name])
        arrays[f"in_{name}_dram"] = a
        args.append(nc.dram_tensor(f"in_{name}_dram", a.shape, _mybir.dt.from_np(a.dtype), kind="ExternalInput").ap())
    for i, (shape, dtype) in enumerate(_OUTS):
        dt = _mybir.dt.from_np(_np.dtype(dtype))
        args.append(nc.dram_tensor(f"out_{i}_dram", shape, dt, kind="ExternalOutput").ap())
    gnn_attention_layernorm_kernel(nc, *args)
    r = _run(nc, [arrays], core_ids=[0])
    got = tuple(r.results[0][f"out_{i}_dram"] for i in range(len(_OUTS)))
    return got[0]
```

```python
import concourse.bass as bass
from concourse import mybir
from contextlib import ExitStack


class Chain:

    def __init__(self, engine, sem, base=0):
        self.engine, self.sem, self.base, self.n = engine, sem, base, 0

    def __call__(self, ins):
        self.n += 1
        ins.then_inc(self.sem, 1)
        self.engine.wait_ge(self.sem, self.base + self.n)


def gnn_attention_layernorm_kernel(
    nc: bass.Bass,
    x: bass.AP,
    adj: bass.AP,
    pairs: bass.AP,
    Wq: bass.AP,
    bq: bass.AP,
    Wk: bass.AP,
    bk: bass.AP,
    out: bass.AP,
):
    fp32, fp16, i32 = mybir.dt.float32, mybir.dt.float16, mybir.dt.int32
    ALU = mybir.AluOpType
    ACT = mybir.ActivationFunctionType
    AX = mybir.AxisListType

    P = 128
    N, H = x.shape
    T = N // P
    HT = H // P
    HEADS = 8
    DK = H // HEADS
    E = pairs.shape[0]
    EC = 80
    EP = E // EC
    assert EP * EC == E and EP <= P
    CH = -(-E // P)
    SELF = 1e-7
    EPS = 1e-5
    LO = 2048.0
    PAST = float(2 * N * N)
    XG = 2
    XP = T // XG
    OG = 2
    MB = 2
    Q = 4
    TQ = T // Q
    SA, SB = 8, 16
    LOOP = (2, 8)
    LAST = T - OG
    assert SA * SB == P and LOOP[0] == OG == MB and (LOOP[1] - LOOP[0]) % OG == 0

    owner = nc.dram_tensor("owner", [N * N, 1], i32, kind="Internal").ap()
    ax_dram = nc.dram_tensor("ax_dram", [N - OG * P, H], fp32, kind="Internal").ap()
    count_dram = nc.dram_tensor("count_dram", [N, 1], fp32, kind="Internal").ap()
    adj_flat = adj.rearrange("a (b o) -> (a b) o", o=1)
    x_tiles = x.rearrange("(t p) h -> p t h", p=P)
    out_tiles = out.rearrange("(t p) h -> p t h", p=P)
    ax_tiles = ax_dram.rearrange("(t p) h -> p t h", p=P)

    ctx = ExitStack()
    with ctx:
        def sb(name, shape, dt=fp32):
            return ctx.enter_context(nc.sbuf_tensor(name, shape, dt))

        def pb(name, shape, dt=fp32):
            return ctx.enter_context(nc.psum_tensor(name, shape, dt))

        ident = sb("ident", [P, P])
        ident16 = sb("ident16", [P, P], fp16)
        offdiag = sb("offdiag", [P, P])
        before = sb("before", [P, P])
        after = sb("after", [P, P])
        ones = sb("ones", [P, P])
        iota_f = sb("iota_f", [P, P])
        iota16 = sb("iota16", [P, SB], fp16)
        slot0 = sb("slot0", [P, 1])
        chunk_lo = sb("chunk_lo", [P, CH])
        self_col = sb("self_col", [P, 1])
        pick_a = sb("pick_a", [P, SA, SB])
        pick_v = sb("pick_v", [P, 3])
        plain_e0 = sb("plain_e0", [P, 1])
        xs = sb("xs", [P, T, H])
        xh = sb("xh", [P, T, H], fp16)
        xl = sb("xl", [P, T, H], fp16)
        adjf = sb("adjf", [P, 2, N])
        mask = sb("mask", [P, MB, N], fp16)
        maskT = sb("maskT", [P, 2, T, P], fp16)
        low_part = sb("low_part", [P, 2, H])
        ax = sb("ax", [P, T, H])
        wraw = ax[:, T - 2 * HT:T, :].rearrange("p (w o) i -> p w o i", w=2)
        count = sb("count", [P, T])
        wT = sb("wT", [P, 2, HT, H])
        bias = sb("bias", [P, 2, H])
        pr = sb("pr", [P, EC, 2], i32)
        prf = sb("prf", [P, EC, 2])
        so16 = sb("so16", [P, EC, 2], fp16)
        keyf = sb("keyf", [P, EC])
        key_i = sb("key_i", [P, EC], i32)
        adjv = sb("adjv", [P, EC])
        act = sb("act", [P, EC])
        incl = sb("incl", [P, EC])
        zeros = sb("zeros", [P, EC])
        slot = sb("slot", [P, EC])
        slot_c = sb("slot_c", [P, EC], i32)
        slot_ab = sb("slot_ab", [P, 2, EC], i32)
        slot_ab16 = sb("slot_ab16", [P, 2, EC], fp16)
        offs = sb("offs", [P, 2])
        nch_f = sb("nch_f", [P, 2])
        nch_i = sb("nch_i", [P, 1], i32)
        chunk_tmp = sb("chunk_tmp", [P, CH])
        area = sb("area", [P, 2560])
        diff = area[:, 0:2 * XG * H].rearrange("p (b n) -> p b n", b=2)
        hot_a = area[:, 0:EC * 3 * SA // 2].bitcast(fp16).rearrange("p (c v a) -> p c v a", v=3, a=SA)
        hot_b = area[:, 1024:1024 + EC * SB // 2].bitcast(fp16).rearrange("p (c b) -> p c b", b=SB)
        picked = area[:, 2048:2048 + P].rearrange("p (a b) -> p a b", a=SA)
        gT = area[:, 0:2 * HT * P].rearrange("p (w k e) -> p w k e", w=2, k=HT)
        attM = area[:, 0:HEADS * P].rearrange("p (h e) -> p h e", h=HEADS)
        qk = area[:, 1024:1024 + 3 * H].rearrange("p (w h) -> p w h", w=3)
        attB = area[:, 1024:1024 + HEADS * P].rearrange("p (h e) -> p h e", h=HEADS)
        wL = area[:, 0:T * P].rearrange("p (t e) -> p t e", t=T)
        g = sb("g", [P, 2, H])
        axg = sb("axg", [P, H])
        se = sb("se", [P, 3])
        si = sb("si", [P, 2], i32)
        split_i = sb("split_i", [P, 2], i32)
        split_f = sb("split_f", [P, 2])
        cols = sb("cols", [P, 24])
        keyv, subv, dup, cnt, rep, uniq = (cols[:, i:i + 1] for i in range(6))
        hiv, lov, objv, slotv, wcol, owned = (cols[:, i:i + 1] for i in range(6, 12))
        skey_f, k2, place_f, row_f, n_edge, c_edge = (cols[:, i:i + 1] for i in range(12, 18))
        d_edge, one, var1, rstd1, early, shift1 = (cols[:, i:i + 1] for i in range(18, 24))
        skey_i = sb("skey_i", [P, 1], i32)
        slot_i = sb("slot_i", [P, 1], i32)
        obj_i = sb("obj_i", [P, 1], i32)
        place_i = sb("place_i", [P, 1], i32)
        row_i = sb("row_i", [P, 1], i32)
        count_g = sb("count_g", [P, 1])
        own_g = sb("own_g", [P, 1], i32)
        own_f = sb("own_f", [P, 1])
        kb = sb("kb", [P, 2, P])
        same = sb("same", [P, P])
        sameW = kb[:, 0, :]
        junk = sb("junk", [P, P])
        att1 = sb("att1", [P, HEADS])
        seg = sb("seg", [P, HEADS])
        hot_lo = sb("hot_lo", [P, P])
        hot_hi = sb("hot_hi", [P, T])
        hot_loT = sb("hot_loT", [P, P])
        last_hot = sb("last_hot", [P, OG, P])
        last_rep = sb("last_rep", [P, OG, P])
        last_w = sb("last_w", [P, OG, P])
        none = sb("none", [P, OG])
        cl = sb("cl", [P, OG])
        dl = sb("dl", [P, OG])
        cl_lo = sb("cl_lo", [P, OG])
        spread = sb("spread", [P, T, HEADS + 1])
        spread8 = sb("spread8", [P, T, HEADS])
        e9 = sb("e9", [P, HEADS + 1])
        dlt = sb("dlt", [P, HEADS])
        pexp = sb("pexp", [P, HEADS])
        x0 = sb("x0", [P, HEADS])
        x1 = sb("x1", [P, HEADS])
        xz = sb("xz", [P, HEADS])
        st1 = sb("st1", [P, 6])
        mv1 = sb("mv1", [P, 2])
        att_all = sb("att_all", [P, CH, HEADS])
        p_all = sb("p_all", [P, CH, HEADS])
        col_all = sb("col_all", [P, CH, 6])
        m_st = sb("m_st", [P, T, HEADS])
        z_st = sb("z_st", [P, T, HEADS + 1])
        rz_st = sb("rz_st", [P, T, HEADS + 1])
        e0 = sb("e0", [P, T, HEADS])
        e1 = sb("e1", [P, T, HEADS])
        rt = sb("rt", [P, T, HEADS])
        n0 = sb("n0", [P, T])
        d1 = sb("d1", [P, T])
        zc = sb("zc", [P, OG])
        cc = sb("cc", [P, OG])
        dc = sb("dc", [P, OG])
        yb = sb("yb", [P, OG, H])
        yl = sb("yl", [P, OG, H])
        stl = sb("stl", [P, OG, 6])
        mvl = sb("mvl", [P, OG, 2])
        stdl = sb("stdl", [P, OG])
        shiftl = sb("shiftl", [P, 1])
        stats = sb("stats", [P, OG, 6])
        mv = sb("mv", [P, OG, 2])
        std = sb("std", [P, OG])
        rstd = sb("rstd", [P, OG])
        shift = sb("shift", [P, OG])

        tp = [pb(f"tp{i}", [P, TQ, P]) for i in range(2)]
        hi_ps = [pb(f"hi_ps{i}", [P, H]) for i in range(2)]
        lo_ps = [pb(f"lo_ps{i}", [P, H]) for i in range(2)]
        ea = pb("ea", [P, H])
        eb = pb("eb", [P, H])

        names = """pairs_in adj_in0 adj_in1 w_in bias_in const_pool const_dve plain_done
            xh_done diff_done xl_done0 xl_done1 w_tr w_copied keys_done adjv_in
            mask_done tr_done copy_done mm_done low_done ax_done cd_done t1_done var_done std_done norm_ready
            norm_done yb_free out_done ax_out count_out
            act_sum_done offs_done nch_done
            f_hots_done f_compact_done f_picked_done f_chosen_done f_idx_done f_sub_rows_in f_obj_rows_in f_kb_done f_keyT_done f_keyT_used
            f_subT_done f_subT_copied f_objT_done f_objT_copied f_q_done f_k_done f_attB_done f_attT_done
            f_place_done f_count_in f_seg_done f_exp_done f_e9_done f_z_done f_sameW_done f_edges_done f_pre_done
            f_ax_in f_var_done f_std_done f_shift_done f_row_done f_row_out
            l_halves_done l_cols_done l_edges_done l_shift_done l_var_done l_std_done l_norm_done l_out_done
            hots_done compact_done picked_done chosen_done idx_done sub_rows_in obj_rows_in kb_done keyT_done keyT_used skey_done
            owner_out subT_done subT_copied objT_done objT_copied q_done k_done attB_done attT_done
            maxspread_done max_done
            hotlo_done hotloT_done hotloT_copied mG_done dlt_done exp_done zspread_done z_done key2_done owner_in
            m_final row_exp_done d1_done scaled_done
            obj2_done obj2_rows_in rzG_done wL_done edge_mm_done edge_added hotlo3_done hotloT3_done hotloT3_copied
            g_var_done g_std_done g_norm_ready g_act_norm_done g_dve_norm_done g_out_done
            dve_setup dve_tile dve_plain dve_last dve_flags dve_fast dve_scan dve_exp dve_rows dve_edges dve_norm
            """.split() + [f"x_in{i}" for i in range(XP)]
        S = {n: ctx.enter_context(nc.semaphore(n)) for n in names}

        def tile_of(tensor, t):
            at = tensor[:, t:t + 1, :] if isinstance(t, int) else tensor[:, bass.ds(t, 1), :]
            return at.rearrange("p a h -> p (a h)")

        def flat(ap):
            return ap.rearrange("p a b -> p (a b)")

        def wide(ap, n):
            return ap.unsqueeze(2).to_broadcast([ap.shape[0], ap.shape[1], n])

        def times(ap, n):
            return ap.unsqueeze(1).to_broadcast([ap.shape[0], n, ap.shape[1]])

        block = ctx.enter_context(nc.Block())

        @block.sync
        def _(sp):
            def load_adj(t, b):
                if not isinstance(t, int) or t >= 2:
                    sp.wait_ge(S["mask_done"], t - 1)
                rows = adj[t * P:(t + 1) * P, :] if isinstance(t, int) else adj[bass.ds(t * P, P), :]
                sp.dma_start(adjf[:, b, :], rows).then_inc(S[f"adj_in{b}"], 16)

            def load_x(i):
                sp.dma_start(xs[:, i * XG:(i + 1) * XG, :],
                             x_tiles[:, i * XG:(i + 1) * XG, :]).then_inc(S[f"x_in{i}"], 16)

            def store_ax(t, n):
                sp.wait_ge(S["ax_done"], t + n + 2)
                at = slice(t, t + n) if isinstance(t, int) else bass.ds(t, n)
                sp.dma_start(ax_tiles[:, at, :], ax[:, at, :]).then_inc(S["ax_out"], 16)

            def store_pair(t):
                number = t // OG
                sp.wait_ge(S["norm_done"], number + 2)
                at = slice(t, t + OG) if isinstance(t, int) else bass.ds(t, OG)
                sp.dma_start(out_tiles[:, at, :], yb[:, :, :]).then_inc(S["out_done"], 16)
                sp.wait_ge(S["out_done"], 16 * (number + 1))
                sp.nop().then_inc(S["yb_free"], 1)

            sp.dma_start(pr[0:EP], pairs.rearrange("(p c) w -> p c w", p=EP)).then_inc(S["pairs_in"], 16)
            for t in range(OG):
                load_adj(t, t)
            for i in range(XP):
                load_x(i)
            for t in range(OG, 2 * OG):
                load_adj(t, t % 2)
            for w, src in enumerate((Wq, Wk)):
                if w == 1:
                    load_adj(4, 0)
                    load_adj(5, 1)
                sp.dma_start(wraw[:, w, :, :], src.rearrange("(o p) i -> p o i", p=P)).then_inc(S["w_in"], 16)
            for w, src in enumerate((bq, bk)):
                sp.dma_start(bias[:, w, :], src.partition_broadcast(P)).then_inc(S["bias_in"], 16)

            def step(t, i):
                if not isinstance(t, int) or t + 4 < T:
                    load_adj(t + 4, i)
                if i == 0:
                    store_ax(t - OG, OG)
                elif t is not T - 1:
                    store_pair(t - OG - 1)

            with sp.Fori(LOOP[0], LOOP[1] - 1, 2) as t0:
                for i in range(2):
                    step(t0 + i, i)
            for t in range(LOOP[1], T - 1):
                if t == T - 3:
                    sp.wait_ge(S["mask_done"], T)
                    sp.dma_start(count_dram.rearrange("(p t) o -> p (t o)", p=P), count[:, :])\
                        .then_inc(S["count_out"], 16)
                step(t, t % 2)
            store_pair(LAST - OG)
            for i in range(OG):
                sp.wait_ge(S["l_norm_done"], i + 1)
                sp.dma_start(out_tiles[:, LAST + i, :], yl[:, i, :]).then_inc(S["l_out_done"], 16)
            sp.wait_ge(S["l_out_done"], 16 * OG)
            sp.wait_ge(S["f_row_out"], 16)
            nch = sp.value_load(nch_i[0:1, 0:1], min_val=1, max_val=CH)
            with sp.If(nch > 1):
                with sp.Fori(0, T // OG) as k:
                    sp.wait_ge(S["g_act_norm_done"], k + 2)
                    sp.wait_ge(S["g_dve_norm_done"], k + 2)
                    sp.dma_start(out_tiles[:, bass.ds(k * OG, OG), :],
                                 ax[:, bass.ds(k * OG, OG), :]).then_inc(S["g_out_done"], 16)
                sp.wait_ge(S["g_out_done"], 16 * (T // OG))

        @block.gpsimd
        def _(pool):
            def rows(out_, table, index, done):
                pool.indirect_dma_start(
                    out=out_, out_offset=None, in_=table,
                    in_offset=bass.IndirectOffsetOnAxis(ap=index, axis=0)).then_inc(S[done], 16)

            nc.gpsimd.memset(ones[:, :], 1.0).then_inc(S["const_pool"], 1)
            nc.gpsimd.iota(iota_f[:, :], [[1, P]], base=0, channel_multiplier=0,
                           allow_small_or_imprecise_dtypes=True).then_inc(S["const_pool"], 1)
            nc.gpsimd.iota(slot0[:, :], [[0, 1]], base=0, channel_multiplier=1,
                           allow_small_or_imprecise_dtypes=True).then_inc(S["const_pool"], 1)
            nc.gpsimd.iota(chunk_lo[:, :], [[P, CH]], base=0, channel_multiplier=0,
                           allow_small_or_imprecise_dtypes=True).then_inc(S["const_pool"], 1)
            pool.wait_ge(S["const_pool"], 4)
            nc.gpsimd.affine_select(out=ident[:, :], in_=ones[:, :], compare_op=ALU.is_equal, fill=0.0, base=0,
                                    pattern=[[-1, P]], channel_multiplier=1).then_inc(S["const_pool"], 1)
            nc.gpsimd.affine_select(out=offdiag[:, :], in_=ones[:, :], compare_op=ALU.not_equal, fill=0.0, base=0,
                                    pattern=[[-1, P]], channel_multiplier=1).then_inc(S["const_pool"], 1)
            nc.gpsimd.affine_select(out=before[:, :], in_=ones[:, :], compare_op=ALU.is_gt, fill=0.0, base=0,
                                    pattern=[[-1, P]], channel_multiplier=1).then_inc(S["const_pool"], 1)
            nc.gpsimd.affine_select(out=after[:, :], in_=ones[:, :], compare_op=ALU.is_gt, fill=0.0, base=0,
                                    pattern=[[1, P]], channel_multiplier=-1).then_inc(S["const_pool"], 1)
            nc.gpsimd.memset(pick_a[:, :, :], 0.0).then_inc(S["const_pool"], 1)
            for n in range(3):
                pool.wait_ge(S["const_pool"], 9 + n)
                nc.gpsimd.affine_select(out=pick_a[:, :, :], in_=pick_a[:, :, :], compare_op=ALU.not_equal, fill=1.0,
                                        base=-SA * n, pattern=[[-1, SA], [0, SB]], channel_multiplier=1)\
                    .then_inc(S["const_pool"], 1)
            nc.gpsimd.affine_select(out=pick_v[:, :], in_=ones[:, 0:3], compare_op=ALU.is_ge, fill=0.0, base=0,
                                    pattern=[[-SA, 3]], channel_multiplier=1).then_inc(S["const_pool"], 1)
            pool.wait_ge(S["const_pool"], 13)
            nc.gpsimd.affine_select(out=pick_v[:, :], in_=pick_v[:, :], compare_op=ALU.is_ge, fill=0.0, base=SA - 1,
                                    pattern=[[SA, 3]], channel_multiplier=-1).then_inc(S["const_pool"], 1)
            pool.wait_ge(S["keys_done"], 1)
            for j in range(EC):
                rows(adjv[0:EP, j:j + 1], adj_flat[:, :], key_i[0:EP, j:j + 1], "adjv_in")
            pool.wait_ge(S["f_idx_done"], 1)
            rows(g[:, 0, :], x[:, :], si[:, 0:1], "f_sub_rows_in")
            rows(g[:, 1, :], x[:, :], si[:, 1:2], "f_obj_rows_in")
            pool.wait_ge(S["f_place_done"], 1)
            pool.wait_ge(S["count_out"], 16)
            rows(count_g[:, :], count_dram, place_i[:, :], "f_count_in")
            pool.wait_ge(S["ax_out"], 16 * (LAST // OG))
            pool.indirect_dma_start(
                out=axg[:, :], out_offset=None, in_=ax_dram[:, :],
                in_offset=bass.IndirectOffsetOnAxis(ap=si[:, 0:1], axis=0),
                bounds_check=LAST * P - 1, oob_is_err=False).then_inc(S["f_ax_in"], 16)
            pool.wait_ge(S["f_row_done"], 1)
            pool.wait_ge(S["out_done"], 16 * (LAST // OG))
            pool.indirect_dma_start(
                out=out[:, :], out_offset=bass.IndirectOffsetOnAxis(ap=row_i[:, :], axis=0), in_=g[:, 0, :],
                in_offset=None, bounds_check=N - 1, oob_is_err=False).then_inc(S["f_row_out"], 16)
            pool.wait_ge(S["nch_done"], 1)
            nch = pool.value_load(nch_i[0:1, 0:1], min_val=1, max_val=CH)
            with pool.If(nch > 1):
                last_pair = pool.to_reg(N * N - 1)
                with pool.Fori(1, nch + 1) as turn:
                    pool.wait_ge(S["nch_done"], 1)
                    pool.wait_ge(S["idx_done"], turn)
                    rows(g[:, 0, :], x[:, :], si[:, 0:1], "sub_rows_in")
                    rows(g[:, 1, :], x[:, :], si[:, 1:2], "obj_rows_in")
                    pool.wait_ge(S["nch_done"], 1)
                    pool.wait_ge(S["skey_done"], turn)
                    pool.indirect_dma_start(
                        out=owner, out_offset=bass.IndirectOffsetOnAxis(ap=skey_i[:, :], axis=0), in_=slot_i[:, :],
                        in_offset=None, bounds_check=last_pair, oob_is_err=False).then_inc(S["owner_out"], 16)
                    pool.wait_ge(S["owner_out"], 16 * turn)
                with pool.Fori(1, nch + 1) as turn:
                    pool.wait_ge(S["nch_done"], 1)
                    pool.wait_ge(S["key2_done"], turn)
                    pool.indirect_dma_start(
                        out=own_g[:, :], out_offset=None, in_=owner,
                        in_offset=bass.IndirectOffsetOnAxis(ap=skey_i[:, :], axis=0),
                        bounds_check=last_pair, oob_is_err=False).then_inc(S["owner_in"], 16)
                with pool.Fori(1, nch + 1) as turn:
                    pool.wait_ge(S["nch_done"], 1)
                    pool.wait_ge(S["obj2_done"], turn)
                    rows(g[:, 1, :], x[:, :], obj_i[:, :], "obj2_rows_in")

        @block.scalar
        def _(act_e):
            a = nc.scalar
            act_e.wait_ge(S["const_dve"], 2)
            a.activation(plain_e0[:, :], self_col[:, :], ACT.Exp, scale=-1.0).then_inc(S["plain_done"], 1)
            a.activation(std[:, 0:1], self_col[:, :], ACT.Copy).then_inc(S["norm_done"], 1)
            a.activation(std[:, 1:2], self_col[:, :], ACT.Copy).then_inc(S["g_act_norm_done"], 1)

            def high_x(i):
                act_e.wait_ge(S[f"x_in{i}"], 16)
                a.activation(xh[:, i * XG:(i + 1) * XG, :], xs[:, i * XG:(i + 1) * XG, :], ACT.Copy)\
                    .then_inc(S["xh_done"], 1)

            def low_x(i):
                act_e.wait_ge(S["diff_done"], i + 1)
                a.activation(flat(xl[:, i * XG:(i + 1) * XG, :]), diff[:, 1, :], ACT.Copy, scale=LO)\
                    .then_inc(S["xl_done1"], 1)

            def copy_quarter(t, b, q):
                act_e.wait_ge(S["tr_done"], Q * t + q + 1)
                a.activation(maskT[:, b, q * TQ:(q + 1) * TQ, :], tp[q % 2][:, :, :], ACT.Copy)\
                    .then_inc(S["copy_done"], 1)

            for q in range(Q):
                copy_quarter(0, 0, q)
            high_x(0)
            for q in range(2):
                copy_quarter(1, 1, q)
            high_x(1)
            for i in range(2, XP, 2):
                high_x(i)
                low_x(i - 1)
                if i == 2:
                    for q in range(2, Q):
                        copy_quarter(1, 1, q)
                high_x(i + 1)
            low_x(XP - 1)

            def low_out(t, b):
                act_e.wait_ge(S["mm_done"], t + 1)
                act_e.wait_ge(S["ax_done"], t + 1)
                a.activation(low_part[:, b, :], lo_ps[b][:, :], ACT.Copy, scale=1.0 / LO).then_inc(S["low_done"], 1)

            def scaled_x(t):
                number = t // OG
                act_e.wait_ge(S["cd_done"], number + 1)
                act_e.wait_ge(S["yb_free"], number + 1)
                for i in range(OG):
                    a.activation(yb[:, i, :], tile_of(xs, t + i), ACT.Copy, scale=dc[:, i:i + 1])\
                        .then_inc(S["t1_done"], 1)

            def std_of(t):
                act_e.wait_ge(S["var_done"], t // OG + 1)
                a.activation(std[:, :], mv[:, :, 1], ACT.Sqrt).then_inc(S["std_done"], 1)

            def normalise(t):
                act_e.wait_ge(S["norm_ready"], t // OG + 1)
                for i in range(OG):
                    last = a.activation(yb[:, i, :], yb[:, i, :], ACT.Identity, scale=rstd[:, i:i + 1],
                                        bias=shift[:, i:i + 1])
                last.then_inc(S["norm_done"], 1)

            def step(t, i, hooks={}):
                pair = not (isinstance(t, int) and t < OG)
                for q in range(Q):
                    for hook in hooks.get(q, ()):
                        hook()
                    if pair and (i, q) == (0, 1):
                        scaled_x(t - OG)
                    if pair and (i, q) == (1, 2):
                        normalise(t - OG - 1)
                    if not (isinstance(t, int) and t == T - 1):
                        copy_quarter(t + 1, (i + 1) % 2, q)
                if pair and i == 0:
                    std_of(t - OG)
                for hook in hooks.get("out", ()):
                    hook()
                low_out(t, i)

            def std_last(i):
                act_e.wait_ge(S["l_var_done"], i + 1)
                a.activation(stdl[:, i:i + 1], mvl[:, i, 1:2], ACT.Sqrt).then_inc(S["l_std_done"], 1)

            def copy_weights(q):
                for n in range(2 * HT // Q * q, 2 * HT // Q * (q + 1)):
                    act_e.wait_ge(S["w_tr"], n + 1)
                    a.activation(wT[:, n // HT, n % HT, :], (ea, eb)[n % 2][:, :], ACT.Copy)\
                        .then_inc(S["w_copied"], 1)

            def copy_gathered(w, turn, k=""):
                tr, cp = (("subT_done", "subT_copied"), ("objT_done", "objT_copied"))[w]
                act_e.wait_ge(S[k + tr], turn)
                a.activation(gT[:, w, :, :].rearrange("p k e -> p (k e)"), (ea, eb)[w][:, :], ACT.Copy)\
                    .then_inc(S[k + cp], 1)

            def edge_exps():
                act_e.wait_ge(S["f_seg_done"], 1)
                a.activation(pexp[:, :], dlt[:, :], ACT.Exp).then_inc(S["f_exp_done"], 1)
                a.activation(x0[:, :], seg[:, :], ACT.Exp, scale=-1.0).then_inc(S["f_exp_done"], 1)
                a.activation(x1[:, :], seg[:, :], ACT.Exp, scale=-1.0, bias=self_col[:, 0:1])\
                    .then_inc(S["f_exp_done"], 1)

            for q in range(2):
                copy_quarter(OG, 0, q)
            low_out(0, 0)
            for q in range(2, Q):
                copy_quarter(OG, 0, q)
            low_out(1, 1)
            with act_e.Fori(LOOP[0], LOOP[1] - 1, 2) as t0:
                for i in range(2):
                    step(t0 + i, i)
            ACT_HOOKS = {
                8: {q: [lambda q=q: copy_weights(q)] for q in range(Q)},
                12: {1: [lambda: copy_gathered(0, 1, "f_"), lambda: copy_gathered(1, 1, "f_")]},
                13: {"out": [edge_exps]},
            }
            for t in range(LOOP[1], T - 1):
                step(t, t % 2, ACT_HOOKS.get(t, {}))
            act_e.wait_ge(S["f_var_done"], 1)
            a.activation(rstd1, var1, ACT.Sqrt).then_inc(S["f_std_done"], 1)
            normalise(LAST - OG)
            act_e.wait_ge(S["f_shift_done"], 1)
            a.activation(g[:, 0, :], g[:, 0, :], ACT.Identity, scale=rstd1, bias=shift1).then_inc(S["f_row_done"], 1)
            std_last(0)
            act_e.wait_ge(S["l_shift_done"], 1)
            a.activation(yl[:, 0, :], yl[:, 0, :], ACT.Identity, scale=stdl[:, 0:1], bias=shiftl[:, :])\
                .then_inc(S["l_norm_done"], 1)
            std_last(1)

            act_e.wait_ge(S["nch_done"], 1)
            nch = act_e.value_load(nch_i[0:1, 0:1], min_val=1, max_val=CH)
            with act_e.If(nch > 1):
                with act_e.Fori(0, nch) as c:
                    for w in range(2):
                        copy_gathered(w, c + 1)
                with act_e.Fori(0, nch) as c:
                    act_e.wait_ge(S["dlt_done"], c + 1)
                    a.activation(pexp[:, :], dlt[:, :], ACT.Exp).then_inc(S["exp_done"], 1)
                act_e.wait_ge(S["m_final"], 1)
                a.activation(e0[:, :, :], m_st[:, :, :], ACT.Exp, scale=-1.0).then_inc(S["row_exp_done"], 1)
                a.activation(e1[:, :, :], m_st[:, :, :], ACT.Exp, scale=-1.0,
                             bias=self_col[:, 0:1]).then_inc(S["row_exp_done"], 1)
                act_e.wait_ge(S["d1_done"], 1)
                with act_e.Fori(0, T) as t:
                    a.activation(xs[:, bass.ds(t, 1), :], xs[:, bass.ds(t, 1), :], ACT.Copy,
                                 scale=d1[:, bass.ds(t, 1)]).then_inc(S["scaled_done"], 1)
                with act_e.Fori(0, T // OG) as k:
                    act_e.wait_ge(S["g_var_done"], k + 1)
                    a.activation(std[:, :], mv[:, :, 1], ACT.Sqrt).then_inc(S["g_std_done"], 1)
                    act_e.wait_ge(S["g_norm_ready"], k + 1)
                    a.activation(tile_of(ax, k * OG), yb[:, 0, :], ACT.Identity, scale=rstd[:, 0:1],
                                 bias=shift[:, 0:1]).then_inc(S["g_act_norm_done"], 1)

        @block.tensor
        def _(pe):
            pe.wait_ge(S["const_dve"], 2)
            mm = nc.tensor.matmul

            def transposes(t, b, q):
                if q == 0:
                    pe.wait_ge(S["mask_done"], t + 1)
                if not (isinstance(t, int) and t == 0 and q < 2):
                    pe.wait_ge(S["copy_done"], Q * t + q - 1)
                for j in range(TQ):
                    k = q * TQ + j
                    last = mm(tp[q % 2][:, j, :], mask[:, b, k * P:(k + 1) * P], ident16[:, :], start=True, stop=True)
                last.then_inc(S["tr_done"], 1)

            def products(t, b, q):
                pe.wait_ge(S["copy_done"], Q * t + q + 1)
                if q == 0:
                    pe.wait_ge(S["ax_done"], t + 1)
                for j in range(q * TQ, (q + 1) * TQ):
                    if isinstance(t, int) and t == 0 and j % XG == 0:
                        pe.wait_ge(S[f"xl_done{j // XG % 2}"], j // XG // 2 + 1)
                    mm(hi_ps[b][:, :], maskT[:, b, j, :], xh[:, j, :], start=(j == 0), stop=(j == T - 1))
                    last = mm(lo_ps[b][:, :], maskT[:, b, j, :], xl[:, j, :], start=(j == 0), stop=(j == T - 1))
                if q == Q - 1:
                    last.then_inc(S["mm_done"], 1)

            def step(t, i, hooks={}):
                for q in range(Q):
                    for hook in hooks.get(q, ()):
                        hook()
                    if not (isinstance(t, int) and t == T - 1):
                        transposes(t + 1, (i + 1) % MB, q)
                    products(t, i % 2, q)

            def transpose_weights(q):
                pe.wait_ge(S["w_in"], 32)
                for n in range(2 * HT // Q * q, 2 * HT // Q * (q + 1)):
                    if n >= 2:
                        pe.wait_ge(S["w_copied"], n - 1)
                    for o in range(HT):
                        last = nc.tensor.transpose((ea, eb)[n % 2][:, o * P:(o + 1) * P],
                                                   wraw[:, n // HT, o, (n % HT) * P:(n % HT + 1) * P], ident[:, :])
                    last.then_inc(S["w_tr"], 1)

            def slot_offsets():
                pe.wait_ge(S["act_sum_done"], 1)
                pe.wait_ge(S["w_copied"], 2 * HT)
                mm(eb[:, 0:1], after[0:EP, :], incl[0:EP, EC - 1:EC], start=True, stop=True)
                mm(eb[:, 1:2], ones[0:EP, :], incl[0:EP, EC - 1:EC], start=True, stop=True)\
                    .then_inc(S["offs_done"], 1)

            def compact(turn, k=""):
                pe.wait_ge(S[k + "hots_done"], turn)
                for n in range(EC):
                    last = mm(ea[0:3 * SA, 0:SB], hot_a[0:EP, n, :, :].rearrange("p v a -> p (v a)"),
                              hot_b[0:EP, n, :], start=(n == 0), stop=(n == EC - 1))
                last.then_inc(S[k + "compact_done"], 1)

            def choose(turn, k=""):
                pe.wait_ge(S[k + "picked_done"], turn)
                mm(eb[:, 0:3], picked[0:3 * SA, :, :].rearrange("p a b -> p (a b)"), pick_v[0:3 * SA, :],
                   start=True, stop=True).then_inc(S[k + "chosen_done"], 1)

            def keys_across(turn, k=""):
                pe.wait_ge(S[k + "kb_done"], turn)
                for w in range(2):
                    last = nc.tensor.transpose(eb[:, w * P:(w + 1) * P], kb[:, w, :], ident[:, :])
                last.then_inc(S[k + "keyT_done"], 1)

            def gathered_across(w, turn, k=""):
                pe.wait_ge(S[k + ("sub_rows_in", "obj_rows_in")[w]], 16 * turn)
                if w == 1:
                    pe.wait_ge(S[k + "keyT_used"], turn)
                for i in range(HT):
                    last = nc.tensor.transpose((ea, eb)[w][:, i * P:(i + 1) * P], g[:, w, i * P:(i + 1) * P],
                                               ident[:, :])
                last.then_inc(S[k + ("subT_done", "objT_done")[w]], 1)

            def project(w, turn, k=""):
                pe.wait_ge(S[k + ("subT_copied", "objT_copied")[w]], turn)
                for i in range(HT):
                    last = mm((ea, eb)[w][:, :], gT[:, w, i, :], wT[:, w, i, :], start=(i == 0), stop=(i == HT - 1))
                last.then_inc(S[k + ("q_done", "k_done")[w]], 1)

            def scores_across(turn, k=""):
                pe.wait_ge(S[k + "attB_done"], turn)
                for h in range(HEADS):
                    ps = (ea, eb)[h // 4]
                    last = nc.tensor.transpose(ps[:, (h % 4) * P:(h % 4 + 1) * P], attB[:, h, :], ident[:, :])
                last.then_inc(S[k + "attT_done"], 1)

            def edge_sums():
                pe.wait_ge(S["f_e9_done"], 1)
                mm(ea[:, 0:HEADS + 1], same[:, :], e9[:, :], start=True, stop=True).then_inc(S["f_z_done"], 1)

            def edge_rows():
                pe.wait_ge(S["f_sameW_done"], 1)
                mm(eb[:, :], sameW, g[:, 1, :], start=True, stop=True).then_inc(S["f_edges_done"], 1)

            def last_columns():
                pe.wait_ge(S["f_sameW_done"], 1)
                pe.wait_ge(S["copy_done"], Q * T)
                for i in range(OG):
                    last = mm(tp[0][:, i, 0:3], last_rep[:, i, :], cols[:, 17:20], start=True, stop=True)
                last.then_inc(S["l_cols_done"], 1)

            def last_edges(i):
                if i == 1:
                    pe.wait_ge(S["f_pre_done"], 1)
                mm((ea, eb)[i][:, :], last_w[:, i, :], g[:, 1, :], start=True, stop=True)\
                    .then_inc(S["l_edges_done"], 1)

            for t in range(OG):
                for q in range(Q):
                    transposes(t, t, q)
            for q in range(Q):
                for t in range(OG):
                    products(t, t, q)
                    if q == Q - 1:
                        for n in range(2):
                            transposes(OG, 0, 2 * t + n)
            with pe.Fori(LOOP[0], LOOP[1] - 1, 2) as t0:
                for i in range(2):
                    step(t0 + i, i)
            f = "f_"

            def last_products(half):
                if half == 0:
                    pe.wait_ge(S["copy_done"], Q * T)
                    pe.wait_ge(S["ax_done"], T)
                b = (T - 1) % 2
                for j in range(T):
                    last = mm((lo_ps, hi_ps)[half][b][:, :], maskT[:, b, j, :], (xl, xh)[half][:, j, :],
                              start=(j == 0), stop=(j == T - 1))
                last.then_inc(S["l_halves_done"], 1)

            PE_HOOKS = {
                8: {q: [lambda q=q: transpose_weights(q)] for q in range(Q)},
                9: {1: [slot_offsets]},
                10: {2: [lambda: compact(1, f)], 3: [lambda: choose(1, f)]},
                11: {1: [lambda: keys_across(1, f)]},
                12: {1: [lambda: gathered_across(0, 1, f), lambda: gathered_across(1, 1, f)],
                     2: [lambda: project(0, 1, f)], 3: [lambda: project(1, 1, f)]},
                13: {1: [lambda: scores_across(1, f)]},
                14: {1: [edge_sums], 3: [edge_rows]},
            }
            for t in range(LOOP[1], T - 1):
                step(t, t % 2, PE_HOOKS.get(t, {}))
            last_columns()
            last_edges(0)
            last_products(0)
            last_edges(1)
            last_products(1)

            pe.wait_ge(S["nch_done"], 1)
            nch = pe.value_load(nch_i[0:1, 0:1], min_val=1, max_val=CH)
            with pe.If(nch > 1):
                with pe.Fori(0, nch) as c:
                    compact(c + 1)
                    choose(c + 1)
                    keys_across(c + 1)
                    for w in range(2):
                        gathered_across(w, c + 1)
                    for w in range(2):
                        project(w, c + 1)
                    scores_across(c + 1)
                    pe.wait_ge(S["maxspread_done"], c + 1)
                    mm(ea[:, 0:T * HEADS], hot_lo[:, :], flat(spread8[:, :, :]),
                       start=True, stop=True).then_inc(S["max_done"], 1)
                with pe.Fori(0, nch) as c:
                    pe.wait_ge(S["hotlo_done"], c + 1)
                    nc.tensor.transpose(eb[:, 0:P], hot_lo[:, :], ident[:, :]).then_inc(S["hotloT_done"], 1)
                    pe.wait_ge(S["hotloT_copied"], c + 1)
                    mm(ea[:, 0:T * HEADS], hot_loT[:, :], flat(m_st[:, :, :]),
                       start=True, stop=True).then_inc(S["mG_done"], 1)
                    pe.wait_ge(S["zspread_done"], c + 1)
                    mm(eb[:, 0:T * (HEADS + 1)], hot_lo[:, :], flat(spread[:, :, :]),
                       start=True, stop=True).then_inc(S["z_done"], 1)
                with pe.Fori(0, nch) as c:
                    pe.wait_ge(S["hotlo3_done"], c + 1)
                    nc.tensor.transpose(eb[:, 0:P], hot_lo[:, :], ident[:, :]).then_inc(S["hotloT3_done"], 1)
                    pe.wait_ge(S["hotloT3_copied"], c + 1)
                    mm(ea[:, 0:T * (HEADS + 1)], hot_loT[:, :], flat(rz_st[:, :, :]),
                       start=True, stop=True).then_inc(S["rzG_done"], 1)
                    pe.wait_ge(S["wL_done"], c + 1)
                    pe.wait_ge(S["obj2_rows_in"], 16 * (c + 1))
                    for t in range(T):
                        if t >= 2:
                            pe.wait_ge(S["edge_added"], c * T + t - 1)
                        mm((ea, eb)[t % 2][:, :], wL[:, t, :], g[:, 1, :], start=True, stop=True)\
                            .then_inc(S["edge_mm_done"], 1)

        @block.vector
        def _(dve):
            v = nc.vector
            setup = Chain(dve, S["dve_setup"])
            v.memset(self_col[:, :], SELF).then_inc(S["const_dve"], 1)
            v.memset(zeros[:, :], 0.0).then_inc(S["ax_done"], 2)
            v.memset(own_g[:, :], -1).then_inc(S["yb_free"], 1)
            v.memset(m_st[:, :, :], SELF).then_inc(S["g_dve_norm_done"], 1)
            v.memset(z_st[:, :, :], 0.0)
            v.memset(one, 1.0)
            setup(v.memset(axg[:, :], 0.0))
            dve.wait_ge(S["pairs_in"], 16)
            setup(v.tensor_copy(prf[0:EP], pr[0:EP]))
            setup(v.scalar_tensor_tensor(out=keyf[0:EP], in0=prf[0:EP, :, 0], scalar=float(N), in1=prf[0:EP, :, 1],
                                         op0=ALU.mult, op1=ALU.add))
            v.tensor_copy(key_i[0:EP], keyf[0:EP]).then_inc(S["keys_done"], 1)
            v.tensor_copy(so16[0:EP, :, 0:2], prf[0:EP])
            dve.wait_ge(S["const_pool"], 14)
            v.tensor_copy(iota16[:, :], iota_f[:, 0:SB])
            v.tensor_copy(ident16[:, :], ident[:, :]).then_inc(S["const_dve"], 1)

            def make_mask(t, i, link):
                b = i % 2
                dve.wait_ge(S[f"adj_in{b}"], 8 * (t - b) + 16)
                diag = adjf[:, b, t * P:(t + 1) * P] if isinstance(t, int) else adjf[:, b, bass.ds(t * P, P)]
                link(v.tensor_tensor(diag, diag, offdiag[:, :], ALU.mult))
                if not isinstance(t, int) or t >= MB:
                    dve.wait_ge(S["tr_done"], Q * (t - MB + 1))
                n = count[:, t:t + 1] if isinstance(t, int) else count[:, bass.ds(t, 1)]
                v.tensor_scalar(mask[:, i % MB, :], adjf[:, b, :], 1.0, 0.0, ALU.is_equal, ALU.add, accum_out=n)\
                    .then_inc(S["mask_done"], 1)

            def sum_halves(t, b):
                dve.wait_ge(S["low_done"], t + 1)
                v.tensor_tensor(tile_of(ax, t), hi_ps[b][:, :], low_part[:, b, :], ALU.add)\
                    .then_inc(S["ax_done"], 1)

            PLAIN = 7

            def plain_weights(t, link):
                dve.wait_ge(S["mask_done"], t + OG)
                n = count[:, t:t + OG] if isinstance(t, int) else count[:, bass.ds(t, OG)]
                link(v.tensor_scalar(zc[:, :], n, plain_e0[:, 0:1], 1.0, ALU.mult, ALU.add))
                link(v.reciprocal(zc[:, :], zc[:, :]))
                v.tensor_scalar(cc[:, :], zc[:, :], plain_e0[:, 0:1], None, ALU.mult)
                v.tensor_scalar(dc[:, :], zc[:, :], 1.0, None, ALU.add).then_inc(S["cd_done"], 1)

            def plain_rows(t, link):
                dve.wait_ge(S["ax_done"], t + OG + 2)
                for i in range(OG):
                    dve.wait_ge(S["t1_done"], t + i + 1)
                    ins = v.scalar_tensor_tensor(out=yb[:, i, :], in0=tile_of(ax, t + i), scalar=cc[:, i:i + 1],
                                                 in1=yb[:, i, :], op0=ALU.mult, op1=ALU.add)
                link(ins)
                for i in range(OG):
                    ins = v.bn_stats(stats[:, i, :], yb[:, i, :])
                link(ins)
                v.memset(junk[:, 0:1], 0.0)
                for i in range(OG):
                    ins = v.bn_aggr(mv[:, i, :], stats[:, i, :])
                link(ins)
                v.tensor_scalar(mv[:, :, 1], mv[:, :, 1], EPS, None, ALU.add).then_inc(S["var_done"], 1)

            def plain_scale(t, link):
                dve.wait_ge(S["std_done"], t // OG + 1)
                dve.wait_ge(S["norm_done"], t // OG + 1)
                link(v.reciprocal(rstd[:, :], std[:, :]))
                link(v.tensor_tensor(shift[:, :], mv[:, :, 0], rstd[:, :], ALU.mult))
                v.tensor_scalar(shift[:, :], shift[:, :], -1.0, None, ALU.mult).then_inc(S["norm_ready"], 1)

            def pair_chain(t, n):
                return Chain(dve, S["dve_plain"], t // OG * PLAIN + n)

            def step(t, i, hooks={}):
                pair = not (isinstance(t, int) and t < OG)
                for hook in hooks.get("first", ()):
                    hook()
                if pair and i == 1:
                    plain_scale(t - OG - 1, pair_chain(t - OG - 1, 5))
                if not (isinstance(t, int) and t + MB >= T):
                    make_mask(t + MB, i, Chain(dve, S["dve_tile"], t + MB))
                for hook in hooks.get("mid", ()):
                    hook()
                if pair and i == 0:
                    plain_rows(t - OG, pair_chain(t - OG, 2))
                if i == 1:
                    plain_weights(t - 1, pair_chain(t - 1, 0))
                for hook in hooks.get("sum", ()):
                    hook()
                sum_halves(t, i)

            lastc = Chain(dve, S["dve_last"])

            def statistics_last(i):
                lastc(v.bn_stats(stl[:, i, :], yl[:, i, :]))
                lastc(v.bn_aggr(mvl[:, i, :], stl[:, i, :]))
                v.tensor_scalar(mvl[:, i, 1:2], mvl[:, i, 1:2], EPS, None, ALU.add).then_inc(S["l_var_done"], 1)

            def last_columns():
                dve.wait_ge(S["l_cols_done"], 1)
                lastc(v.tensor_scalar(none[:, :], tp[0][:, 0:OG, 2], -1.0, 1.0, ALU.mult, ALU.add))
                v.tensor_tensor(cl[:, :], cc[:, :], none[:, :], ALU.mult)
                lastc(v.tensor_tensor(dl[:, :], dc[:, :], none[:, :], ALU.mult))
                v.tensor_tensor(cl[:, :], cl[:, :], tp[0][:, 0:OG, 0], ALU.add)
                lastc(v.tensor_tensor(dl[:, :], dl[:, :], tp[0][:, 0:OG, 1], ALU.add))
                lastc(v.tensor_scalar(cl_lo[:, :], cl[:, :], 1.0 / LO, None, ALU.mult))

            def last_x(i):
                dve.wait_ge(S["l_edges_done"], i + 1)
                lastc(v.scalar_tensor_tensor(out=yl[:, i, :], in0=xs[:, LAST + i, :], scalar=dl[:, i:i + 1],
                                             in1=(ea, eb)[i][:, :], op0=ALU.mult, op1=ALU.add))

            def last_add(i, part, scale):
                lastc(v.scalar_tensor_tensor(out=yl[:, i, :], in0=part, scalar=scale[:, i:i + 1],
                                             in1=yl[:, i, :], op0=ALU.mult, op1=ALU.add))

            def last_stds(i):
                dve.wait_ge(S["l_std_done"], i + 1)
                lastc(v.reciprocal(stdl[:, i:i + 1], stdl[:, i:i + 1]))

            def last_tiles():
                b = (T - 1) % 2
                plain_scale(LAST - OG, pair_chain(LAST - OG, 5))
                row_shifts()
                last_columns()
                last_x(0)
                dve.wait_ge(S["ax_done"], LAST + 3)
                last_add(0, ax[:, LAST, :], cl)
                statistics_last(0)
                last_x(1)
                last_stds(0)
                v.tensor_scalar(shiftl[:, :], mvl[:, 0, 0:1], stdl[:, 0:1], -1.0, ALU.mult, ALU.mult)\
                    .then_inc(S["l_shift_done"], 1)
                dve.wait_ge(S["l_halves_done"], 1)
                last_add(1, lo_ps[b][:, :], cl_lo)
                dve.wait_ge(S["l_halves_done"], 2)
                last_add(1, hi_ps[b][:, :], cl)
                statistics_last(1)
                last_stds(1)
                dve.wait_ge(S["l_norm_done"], 1)
                v.tensor_scalar(yl[:, 1, :], yl[:, 1, :], mvl[:, 1, 0:1], stdl[:, 1:2], ALU.subtract, ALU.mult)\
                    .then_inc(S["l_norm_done"], 1)

            valid = se[:, 2:3]

            def one_hots(step_, k=""):
                step_(v.tensor_scalar(slot_c[0:EP], slot[0:EP], -1.0, float(P), ALU.max, ALU.min))
                v.tensor_scalar(slot_ab[0:EP, 0, :], slot_c[0:EP], 4, None, ALU.arith_shift_right)
                step_(v.tensor_scalar(slot_ab[0:EP, 1, :], slot_c[0:EP], SB - 1, None, ALU.bitwise_and))
                step_(v.tensor_copy(slot_ab16[0:EP], slot_ab[0:EP]))
                v.tensor_tensor(hot_b[0:EP], times(iota16[0:EP, :], EC), wide(slot_ab16[0:EP, 1, :], SB), ALU.is_equal)
                step_(v.tensor_tensor(hot_a[0:EP, :, 2, :], times(iota16[0:EP, 0:SA], EC),
                                      wide(slot_ab16[0:EP, 0, :], SA), ALU.is_equal))
                for w in range(2):
                    ins = v.tensor_tensor(hot_a[0:EP, :, w, :], hot_a[0:EP, :, 2, :], wide(so16[0:EP, :, w], SA),
                                          ALU.mult)
                ins.then_inc(S[k + "hots_done"], 1)

            def pick(turn, k=""):
                dve.wait_ge(S[k + "compact_done"], turn)
                v.tensor_tensor(picked[0:3 * SA], pick_a[0:3 * SA], times(ea[0:3 * SA, 0:SB], SA), ALU.mult)\
                    .then_inc(S[k + "picked_done"], 1)

            def locate(step_, turn, k=""):
                dve.wait_ge(S[k + "chosen_done"], turn)
                step_(v.tensor_copy(se[:, :], eb[:, 0:3]))
                step_(v.tensor_copy(si[:, :], se[:, 0:2]))
                v.scalar_tensor_tensor(out=keyv, in0=se[:, 0:1], scalar=float(N), in1=se[:, 1:2],
                                       op0=ALU.mult, op1=ALU.add).then_inc(S[k + "idx_done"], 1)
                v.tensor_scalar(split_i[:, 0:1], si[:, 0:1], 7, None, ALU.arith_shift_right)
                step_(v.tensor_scalar(split_i[:, 1:2], si[:, 0:1], P - 1, None, ALU.bitwise_and))
                step_(v.tensor_copy(split_f[:, :], split_i[:, :]))
                v.tensor_scalar(keyv, keyv, 1.0, valid, ALU.add, ALU.mult)
                v.tensor_scalar(subv, se[:, 0:1], 1.0, valid, ALU.add, ALU.mult)
                step_(v.tensor_scalar(hiv, split_f[:, 0:1], 1.0, valid, ALU.add, ALU.mult))
                step_(v.tensor_scalar(cols[:, 0:2], cols[:, 0:2], -1.0, None, ALU.add))
                step_(v.tensor_scalar(hiv, hiv, -1.0, None, ALU.add))
                v.tensor_copy(kb[:, :, :], wide(cols[:, 0:2], P)).then_inc(S[k + "kb_done"], 1)

            def repeats(step_, turn, k=""):
                dve.wait_ge(S[k + "keyT_done"], turn)
                step_(v.scalar_tensor_tensor(out=junk[:, :], in0=eb[:, 0:P], scalar=keyv, in1=before[:, :],
                                             op0=ALU.is_equal, op1=ALU.mult, accum_out=dup))
                v.tensor_scalar(same[:, :], eb[:, P:2 * P], subv, None, ALU.is_equal).then_inc(S[k + "keyT_used"], 1)
                dve.wait_ge(S[k + "keyT_used"], turn)
                step_(v.scalar_tensor_tensor(out=junk[:, :], in0=same[:, :], scalar=1.0, in1=before[:, :],
                                             op0=ALU.mult, op1=ALU.mult, accum_out=cnt))
                v.tensor_scalar(uniq, dup, 0.0, valid, ALU.is_equal, ALU.mult)
                step_(v.tensor_scalar(rep, cnt, 0.0, valid, ALU.is_equal, ALU.mult))

            def score(step_, turn, k=""):
                for w, done in enumerate(("q_done", "k_done")):
                    dve.wait_ge(S[k + done], turn)
                    ins = v.tensor_tensor(qk[:, w, :], (ea, eb)[w][:, :], bias[:, w, :], ALU.add)
                step_(ins)
                step_(v.tensor_tensor(qk[:, 2, :], qk[:, 0, :], qk[:, 1, :], ALU.mult))
                step_(v.tensor_reduce(att1[:, :], qk[:, 2, :].rearrange("p (h d) -> p h d", h=HEADS), AX.X, ALU.add))
                step_(v.tensor_scalar(att1[:, :], att1[:, :], DK ** -0.5, valid, ALU.mult, ALU.mult))
                v.tensor_copy(attB[:, :, :], wide(att1[:, :], P)).then_inc(S[k + "attB_done"], 1)

            def largest(step_, turn, k=""):
                dve.wait_ge(S[k + "attT_done"], turn)
                for i, ps in enumerate((ea, eb)):
                    ins = v.tensor_tensor(attM[:, 4 * i:4 * i + 4, :], ps[:, :].rearrange("p (h e) -> p h e", h=4),
                                          times(same[:, :], 4), ALU.mult)
                step_(ins)
                step_(v.tensor_reduce(seg[:, :], attM[:, :, :], AX.X, ALU.max))

            fast = Chain(dve, S["dve_fast"])
            f = "f_"

            def find_active():
                fast(v.tensor_tensor(act[0:EP], prf[0:EP, :, 0], prf[0:EP, :, 1], ALU.not_equal))
                dve.wait_ge(S["adjv_in"], 16 * EC)
                fast(v.scalar_tensor_tensor(out=act[0:EP], in0=adjv[0:EP], scalar=1.0, in1=act[0:EP],
                                            op0=ALU.is_equal, op1=ALU.mult))
                v.tensor_tensor_scan(out=incl[0:EP], data0=act[0:EP], data1=zeros[0:EP], initial=0.0,
                                     op0=ALU.add, op1=ALU.add).then_inc(S["act_sum_done"], 1)

            def make_slots():
                dve.wait_ge(S["offs_done"], 1)
                fast(v.tensor_copy(offs[:, :], eb[:, 0:2]))
                fast(v.tensor_scalar(chunk_tmp[:, :], chunk_lo[:, :], offs[:, 1:2], 0.0, ALU.is_lt, ALU.add,
                                     accum_out=nch_f[:, 0:1]))
                v.tensor_scalar(nch_f[:, 1:2], nch_f[:, 0:1], 1.0, None, ALU.max)
                fast(v.tensor_scalar(slot[0:EP], incl[0:EP], offs[0:EP, 0:1], None, ALU.add))
                v.tensor_copy(nch_i[:, :], nch_f[:, 1:2]).then_inc(S["nch_done"], 1)
                fast(v.tensor_tensor(slot[0:EP], slot[0:EP], act[0:EP], ALU.mult))
                fast(v.tensor_scalar(slot[0:EP], slot[0:EP], -1.0, None, ALU.add))
                one_hots(fast, f)

            def place_rows():
                locate(fast, 1, f)
                fast(v.scalar_tensor_tensor(out=place_f, in0=split_f[:, 1:2], scalar=float(T), in1=split_f[:, 0:1],
                                            op0=ALU.mult, op1=ALU.add))
                v.tensor_copy(place_i[:, :], place_f).then_inc(S["f_place_done"], 1)

            def find_repeats():
                repeats(fast, 1, f)
                for i in range(OG):
                    v.tensor_scalar(last_hot[:, i, :], iota_f[:, :], float((LAST + i) * P), subv,
                                    ALU.add, ALU.is_equal)
                fast(v.tensor_scalar(early, subv, float(LAST * P), rep, ALU.is_lt, ALU.mult))
                v.tensor_scalar(flat(last_rep[:, :, :]), flat(last_hot[:, :, :]), rep, None, ALU.mult)
                fast(v.tensor_scalar(row_f, early, -PAST, PAST, ALU.mult, ALU.add))
                fast(v.tensor_tensor(row_f, row_f, se[:, 0:1], ALU.add))
                fast(v.tensor_copy(row_i[:, :], row_f))

            def row_maximum():
                largest(fast, 1, f)
                fast(v.tensor_scalar(seg[:, :], seg[:, :], SELF, None, ALU.max))
                v.tensor_tensor(dlt[:, :], att1[:, :], seg[:, :], ALU.subtract).then_inc(S["f_seg_done"], 1)
                v.tensor_copy(e9[:, HEADS:HEADS + 1], uniq)

            def edge_weights():
                dve.wait_ge(S["f_exp_done"], 3)
                v.tensor_scalar(e9[:, 0:HEADS], pexp[:, :], uniq, None, ALU.mult).then_inc(S["f_e9_done"], 1)

            def row_weights():
                dve.wait_ge(S["f_z_done"], 1)
                dve.wait_ge(S["f_e9_done"], 1)
                dve.wait_ge(S["f_count_in"], 16)
                fast(v.tensor_tensor(n_edge, count_g[:, :], ea[:, HEADS:HEADS + 1], ALU.subtract))
                fast(v.scalar_tensor_tensor(out=xz[:, :], in0=x0[:, :], scalar=n_edge, in1=x1[:, :],
                                            op0=ALU.mult, op1=ALU.add))
                fast(v.tensor_tensor(xz[:, :], xz[:, :], ea[:, 0:HEADS], ALU.add))
                fast(v.reciprocal(xz[:, :], xz[:, :]))
                fast(v.tensor_scalar(xz[:, :], xz[:, :], 1.0 / HEADS, None, ALU.mult))
                v.scalar_tensor_tensor(out=x0[:, :], in0=x0[:, :], scalar=1.0, in1=xz[:, :], op0=ALU.mult,
                                       op1=ALU.mult, accum_out=c_edge)
                v.scalar_tensor_tensor(out=x1[:, :], in0=x1[:, :], scalar=1.0, in1=xz[:, :], op0=ALU.mult,
                                       op1=ALU.mult, accum_out=d_edge)
                fast(v.scalar_tensor_tensor(out=dlt[:, :], in0=e9[:, 0:HEADS], scalar=1.0, in1=xz[:, :],
                                            op0=ALU.mult, op1=ALU.mult, accum_out=wcol))
                v.tensor_scalar(d_edge, d_edge, 1.0, None, ALU.add)
                fast(v.tensor_scalar(wcol, wcol, c_edge, uniq, ALU.subtract, ALU.mult))
                v.tensor_scalar(flat(last_w[:, :, :]), flat(last_hot[:, :, :]), wcol, None, ALU.mult)
                v.tensor_scalar(sameW, same[:, :], wcol, None, ALU.mult).then_inc(S["f_sameW_done"], 1)

            def rows_but_ax():
                dve.wait_ge(S["f_edges_done"], 1)
                v.scalar_tensor_tensor(out=g[:, 0, :], in0=g[:, 0, :], scalar=d_edge, in1=eb[:, :],
                                       op0=ALU.mult, op1=ALU.add).then_inc(S["f_pre_done"], 1)

            def finish_rows():
                dve.wait_ge(S["f_pre_done"], 1)
                dve.wait_ge(S["f_ax_in"], 16)
                fast(v.scalar_tensor_tensor(out=g[:, 0, :], in0=axg[:, :], scalar=c_edge, in1=g[:, 0, :],
                                            op0=ALU.mult, op1=ALU.add))
                fast(v.bn_stats(st1[:, :], g[:, 0, :]))
                fast(v.bn_aggr(mv1[:, :], st1[:, :]))
                v.tensor_scalar(var1, mv1[:, 1:2], EPS, None, ALU.add).then_inc(S["f_var_done"], 1)

            def row_shifts():
                dve.wait_ge(S["f_std_done"], 1)
                fast(v.reciprocal(rstd1, rstd1))
                v.tensor_scalar(shift1, mv1[:, 0:1], rstd1, -1.0, ALU.mult, ALU.mult).then_inc(S["f_shift_done"], 1)

            tile = Chain(dve, S["dve_tile"])
            for t in range(OG):
                make_mask(t, t, tile)
            for i in range(XP):
                piece = slice(i * XG, (i + 1) * XG)
                dve.wait_ge(S["xh_done"], i + 1)
                if i >= 2:
                    dve.wait_ge(S[f"xl_done{i % 2}"], i // 2)
                v.tensor_tensor(diff[:, i % 2, :], flat(xs[:, piece, :]), flat(xh[:, piece, :]), ALU.subtract)\
                    .then_inc(S["diff_done"], 1)
                if i % 2 == 0:
                    dve.wait_ge(S["diff_done"], i + 1)
                    v.tensor_scalar(flat(xl[:, piece, :]), diff[:, 0, :], LO, None, ALU.mult)\
                        .then_inc(S["xl_done0"], 1)
            dve.wait_ge(S["plain_done"], 1)
            for t in range(OG, 2 * OG):
                make_mask(t, t % 2, Chain(dve, S["dve_tile"], t))
            plain_weights(0, pair_chain(0, 0))
            for t in range(OG):
                sum_halves(t, t)
            with dve.Fori(LOOP[0], LOOP[1] - 1, 2) as t0:
                for i in range(2):
                    step(t0 + i, i)
            DVE_HOOKS = {
                8: {"sum": [find_active, lambda: dve.wait_ge(S["w_copied"], 2 * HT)]},
                9: {"sum": [make_slots]},
                10: {"mid": [lambda: pick(1, f)], "sum": [place_rows]},
                11: {"sum": [find_repeats]},
                12: {"sum": [lambda: score(fast, 1, f)]},
                13: {"mid": [row_maximum]},
                14: {"first": [edge_weights], "mid": [row_weights],
                     "sum": [rows_but_ax, lambda: plain_weights(LAST, lastc), finish_rows]},
            }
            for t in range(LOOP[1], T - 1):
                if t == 11:
                    dve.wait_ge(S["bias_in"], 32)
                step(t, t % 2, DVE_HOOKS.get(t, {}))
            last_tiles()

            dve.wait_ge(S["f_row_out"], 16)
            nch = dve.value_load(nch_i[0:1, 0:1], min_val=1, max_val=CH)

            def column(c, i):
                return flat(col_all[:, bass.ds(c, 1), i:i + 1])

            def heads_of(tensor, c):
                return flat(tensor[:, bass.ds(c, 1), :])

            with dve.If(nch > 1):
                start = Chain(dve, S["dve_flags"])
                start(v.tensor_scalar(low_part[:, 1, :], lo_ps[(T - 1) % 2][:, :], 1.0 / LO, None, ALU.mult))
                start(v.tensor_tensor(ax[:, T - 1, :], hi_ps[(T - 1) % 2][:, :], low_part[:, 1, :], ALU.add))
                start(v.tensor_copy(slotv, slot0[:, :]))
                start(v.tensor_scalar(slot[0:EP], slot[0:EP], float(P), None, ALU.add))
                STEPS1 = 28
                with dve.Fori(0, nch) as c:
                    step1 = Chain(dve, S["dve_scan"], c * STEPS1)
                    step1(v.tensor_scalar(slot[0:EP], slot[0:EP], -float(P), None, ALU.add))
                    one_hots(step1)
                    pick(c + 1)
                    locate(step1, c + 1)
                    v.tensor_copy(column(c, 0), hiv)
                    v.tensor_copy(column(c, 1), split_f[:, 1:2])
                    v.tensor_copy(column(c, 2), se[:, 1:2])
                    v.tensor_copy(column(c, 3), valid)
                    v.tensor_scalar(hot_hi[:, :], iota_f[:, 0:T], hiv, None, ALU.is_equal)
                    step1(v.tensor_scalar(hot_lo[:, :], iota_f[:, :], split_f[:, 1:2], None, ALU.is_equal))
                    repeats(step1, c + 1)
                    step1(v.tensor_scalar(k2, uniq, -PAST, PAST, ALU.mult, ALU.add))
                    step1(v.tensor_tensor(skey_f, keyv, k2, ALU.add))
                    step1(v.tensor_scalar(skey_f, skey_f, -1.0, None, ALU.max))
                    v.tensor_copy(slot_i[:, :], slotv)
                    v.tensor_copy(skey_i[:, :], skey_f).then_inc(S["skey_done"], 1)
                    score(step1, c + 1)
                    v.tensor_copy(heads_of(att_all, c), att1[:, :])
                    largest(step1, c + 1)
                    step1(v.tensor_scalar(seg[:, :], seg[:, :], rep, None, ALU.mult))
                    v.tensor_tensor(spread8[:, :, :], wide(hot_hi[:, :], HEADS), times(seg[:, :], T), ALU.mult)\
                        .then_inc(S["maxspread_done"], 1)
                    dve.wait_ge(S["max_done"], c + 1)
                    step1(v.tensor_tensor(m_st[:, :, :], m_st[:, :, :],
                                          ea[:, 0:T * HEADS].rearrange("p (t h) -> p t h", h=HEADS), ALU.max))
                    dve.wait_ge(S["owner_out"], 16 * (c + 1))
                    step1(v.tensor_scalar(slotv, slotv, float(P), None, ALU.add))
                    assert step1.n == STEPS1, step1.n
                v.tensor_copy(junk[:, 0:1], self_col[:, :]).then_inc(S["m_final"], 1)

                again = Chain(dve, S["dve_exp"])
                again(v.tensor_copy(slotv, slot0[:, :]))
                STEPS2 = 12
                with dve.Fori(0, nch) as c:
                    step2 = Chain(dve, S["dve_exp"], c * STEPS2 + 1)
                    v.tensor_scalar(hot_hi[:, :], iota_f[:, 0:T], column(c, 0), None, ALU.is_equal)
                    v.tensor_scalar(hot_lo[:, :], iota_f[:, :], column(c, 1), None, ALU.is_equal)\
                        .then_inc(S["hotlo_done"], 1)
                    step2(v.scalar_tensor_tensor(out=subv, in0=column(c, 0), scalar=float(P), in1=column(c, 1),
                                                 op0=ALU.mult, op1=ALU.add))
                    step2(v.scalar_tensor_tensor(out=keyv, in0=subv, scalar=float(N), in1=column(c, 2),
                                                 op0=ALU.mult, op1=ALU.add))
                    step2(v.tensor_scalar(k2, column(c, 3), -PAST, PAST, ALU.mult, ALU.add))
                    step2(v.tensor_tensor(skey_f, keyv, k2, ALU.add))
                    v.tensor_copy(skey_i[:, :], skey_f).then_inc(S["key2_done"], 1)
                    dve.wait_ge(S["hotloT_done"], c + 1)
                    v.tensor_copy(hot_loT[:, :], eb[:, 0:P]).then_inc(S["hotloT_copied"], 1)
                    dve.wait_ge(S["mG_done"], c + 1)
                    step2(v.tensor_tensor(spread8[:, :, :], ea[:, 0:T * HEADS].rearrange("p (t h) -> p t h", h=HEADS),
                                          wide(hot_hi[:, :], HEADS), ALU.mult))
                    step2(v.tensor_reduce(seg[:, :], spread8[:, :, :].rearrange("p t h -> p h t"), AX.X, ALU.add))
                    v.tensor_tensor(dlt[:, :], heads_of(att_all, c), seg[:, :], ALU.subtract)\
                        .then_inc(S["dlt_done"], 1)
                    dve.wait_ge(S["owner_in"], 16 * (c + 1))
                    step2(v.tensor_copy(own_f[:, :], own_g[:, :]))
                    step2(v.tensor_tensor(owned, own_f[:, :], slotv, ALU.is_equal))
                    step2(v.tensor_tensor(owned, owned, column(c, 3), ALU.mult))
                    step2(v.tensor_scalar(slotv, slotv, float(P), None, ALU.add))
                    v.tensor_copy(column(c, 5), owned)
                    v.tensor_copy(e9[:, HEADS:HEADS + 1], owned)
                    dve.wait_ge(S["exp_done"], c + 1)
                    step2(v.tensor_scalar(e9[:, 0:HEADS], pexp[:, :], owned, None, ALU.mult))
                    v.tensor_copy(heads_of(p_all, c), e9[:, 0:HEADS])
                    v.tensor_tensor(spread[:, :, :], wide(hot_hi[:, :], HEADS + 1), times(e9[:, :], T), ALU.mult)\
                        .then_inc(S["zspread_done"], 1)
                    dve.wait_ge(S["z_done"], c + 1)
                    step2(v.tensor_tensor(z_st[:, :, :], z_st[:, :, :],
                                          eb[:, 0:T * (HEADS + 1)].rearrange("p (t h) -> p t h", h=HEADS + 1),
                                          ALU.add))
                    assert step2.n == STEPS2, step2.n

                rows = Chain(dve, S["dve_rows"])
                rows(v.tensor_tensor(n0[:, :], count[:, :], z_st[:, :, HEADS], ALU.subtract))
                dve.wait_ge(S["row_exp_done"], 2)
                rows(v.tensor_tensor(rt[:, :, :], e0[:, :, :], wide(n0[:, :], HEADS), ALU.mult))
                rows(v.tensor_tensor(rt[:, :, :], rt[:, :, :], e1[:, :, :], ALU.add))
                rows(v.tensor_tensor(rt[:, :, :], rt[:, :, :], z_st[:, :, 0:HEADS], ALU.add))
                rows(v.reciprocal(rt[:, :, :], rt[:, :, :]))
                rows(v.tensor_scalar(rz_st[:, :, 0:HEADS], rt[:, :, :], 1.0 / HEADS, None, ALU.mult))
                rows(v.tensor_tensor(rt[:, :, :], rz_st[:, :, 0:HEADS], e1[:, :, :], ALU.mult))
                rows(v.tensor_reduce(d1[:, :], rt[:, :, :], AX.X, ALU.add))
                v.tensor_scalar(d1[:, :], d1[:, :], 1.0, None, ALU.add).then_inc(S["d1_done"], 1)
                rows(v.tensor_tensor(e0[:, :, :], rz_st[:, :, 0:HEADS], e0[:, :, :], ALU.mult))
                rows(v.tensor_reduce(rz_st[:, :, HEADS], e0[:, :, :], AX.X, ALU.add))
                dve.wait_ge(S["scaled_done"], T)

                STEPS3 = 6
                with dve.Fori(0, nch) as c:
                    step3 = Chain(dve, S["dve_edges"], c * STEPS3)
                    v.tensor_copy(obj_i[:, :], column(c, 2)).then_inc(S["obj2_done"], 1)
                    v.tensor_scalar(hot_hi[:, :], iota_f[:, 0:T], column(c, 0), None, ALU.is_equal)
                    v.tensor_scalar(hot_lo[:, :], iota_f[:, :], column(c, 1), None, ALU.is_equal)\
                        .then_inc(S["hotlo3_done"], 1)
                    dve.wait_ge(S["hotloT3_done"], c + 1)
                    v.tensor_copy(hot_loT[:, :], eb[:, 0:P]).then_inc(S["hotloT3_copied"], 1)
                    dve.wait_ge(S["rzG_done"], c + 1)
                    step3(v.tensor_tensor(spread[:, :, :],
                                          ea[:, 0:T * (HEADS + 1)].rearrange("p (t h) -> p t h", h=HEADS + 1),
                                          wide(hot_hi[:, :], HEADS + 1), ALU.mult))
                    step3(v.tensor_reduce(e9[:, :], spread[:, :, :].rearrange("p t h -> p h t"), AX.X, ALU.add))
                    step3(v.tensor_tensor(dlt[:, :], heads_of(p_all, c), e9[:, 0:HEADS], ALU.mult))
                    step3(v.tensor_reduce(wcol, dlt[:, :], AX.X, ALU.add))
                    step3(v.tensor_scalar(wcol, wcol, e9[:, HEADS:HEADS + 1], column(c, 5), ALU.subtract, ALU.mult))
                    step3(v.tensor_scalar(hot_hi[:, :], hot_hi[:, :], wcol, None, ALU.mult))
                    v.tensor_tensor(wL[:, :, :], times(hot_lo[:, :], T), wide(hot_hi[:, :], P), ALU.mult)\
                        .then_inc(S["wL_done"], 1)
                    for t in range(T):
                        dve.wait_ge(S["edge_mm_done"], c * T + t + 1)
                        v.tensor_tensor(xs[:, t, :], xs[:, t, :], (ea, eb)[t % 2][:, :], ALU.add)\
                            .then_inc(S["edge_added"], 1)
                    dve.wait_ge(S["edge_added"], c * T + T)
                    assert step3.n == STEPS3, step3.n

                NSTEPS = 5
                with dve.Fori(0, T // OG) as k:
                    step4 = Chain(dve, S["dve_norm"], k * NSTEPS)
                    dve.wait_ge(S["g_act_norm_done"], k + 1)
                    dve.wait_ge(S["g_dve_norm_done"], k + 1)
                    for i in range(OG):
                        t1 = bass.ds(k * OG + i, 1)
                        ins = v.scalar_tensor_tensor(out=yb[:, i, :], in0=tile_of(ax, k * OG + i),
                                                     scalar=flat(rz_st[:, t1, HEADS:HEADS + 1]),
                                                     in1=tile_of(xs, k * OG + i), op0=ALU.mult, op1=ALU.add)
                    step4(ins)
                    for i in range(OG):
                        ins = v.bn_stats(stats[:, i, :], yb[:, i, :])
                    step4(ins)
                    v.memset(junk[:, 0:1], 0.0)
                    for i in range(OG):
                        ins = v.bn_aggr(mv[:, i, :], stats[:, i, :])
                    step4(ins)
                    v.tensor_scalar(mv[:, :, 1], mv[:, :, 1], EPS, None, ALU.add).then_inc(S["g_var_done"], 1)
                    dve.wait_ge(S["g_std_done"], k + 1)
                    step4(v.reciprocal(rstd[:, :], std[:, :]))
                    step4(v.tensor_tensor(shift[:, :], mv[:, :, 0], rstd[:, :], ALU.mult))
                    v.tensor_scalar(shift[:, :], shift[:, :], -1.0, None, ALU.mult).then_inc(S["g_norm_ready"], 1)
                    dve.wait_ge(S["g_norm_ready"], k + 1)
                    v.tensor_scalar(tile_of(ax, k * OG + 1), yb[:, 1, :], rstd[:, 1:2], shift[:, 1:2],
                                    ALU.mult, ALU.add).then_inc(S["g_dve_norm_done"], 1)
                    assert step4.n == NSTEPS, step4.n


_INS = ['x', 'adj', 'L0_gnn_rel_pair_index', 'L0_gnn_Wq', 'L0_gnn_bq', 'L0_gnn_Wk', 'L0_gnn_bk']
_OUTS = [((2048, 512), 'float32')]


def kernel(**inputs):
    import numpy as _np
    import concourse.bacc as _bacc
    from concourse import mybir as _mybir
    from concourse.bass_utils import run_bass_kernel_spmd as _run

    nc = _bacc.Bacc("TRN2", target_bir_lowering=False, num_devices=1)
    arrays, args = {}, []
    for name in _INS:
        a = _np.ascontiguousarray(inputs[name])
        arrays[f"in_{name}_dram"] = a
        args.append(nc.dram_tensor(f"in_{name}_dram", a.shape, _mybir.dt.from_np(a.dtype), kind="ExternalInput").ap())
    for i, (shape, dtype) in enumerate(_OUTS):
        dt = _mybir.dt.from_np(_np.dtype(dtype))
        args.append(nc.dram_tensor(f"out_{i}_dram", shape, dt, kind="ExternalOutput").ap())
    gnn_attention_layernorm_kernel(nc, *args)
    r = _run(nc, [arrays], core_ids=[0])
    got = tuple(r.results[0][f"out_{i}_dram"] for i in range(len(_OUTS)))
    return got[0]
```
